# Optimizing a Trainium2 kernel written in Bass

```python
import numpy as np
import jax
import jax.numpy as jnp

def _softmax(x, axis=-1):
    return jax.nn.softmax(x, axis=axis)

def _gelu(x):
    return jax.nn.gelu(x, approximate=True)

def _silu(x):
    return jax.nn.silu(x)

def _sigmoid(x):
    return jax.nn.sigmoid(x)

def _layernorm(x, axis=-1, eps=1e-05):
    m = jnp.mean(x, axis=axis, keepdims=True)
    v = jnp.var(x, axis=axis, keepdims=True)
    return (x - m) / jnp.sqrt(v + eps)

def _scatter_add(tgt, idx, src, axis=0):
    return tgt.at[idx].add(src)

def _segment_sum(src, seg, n):
    return jax.ops.segment_sum(src, seg, n)
kernel_name = 'mk_adaln_ffn_d1_seqx_r8_630922'

def setup_inputs(seed: int=0):
    np.random.seed(seed)
    _w = jnp.asarray

    def _rec_inputs():
        import jax
        import jax.numpy as jnp
        _rk = jax.random.key(seed)
        x = -0.0003929 + 0.9999 * jax.random.normal(jax.random.fold_in(_rk, 1), (128, 32, 512), jnp.float32)
        _lenS = 32 - jax.random.randint(jax.random.fold_in(_rk, 7), (128,), 0, max(1, 32 // 4) + 1, jnp.int32)
        _lenS2 = 32 - jax.random.randint(jax.random.fold_in(_rk, 8), (128,), 0, max(1, 32 // 4) + 1, jnp.int32)
        itok_B_8_3872 = jax.random.randint(jax.random.fold_in(_rk, 11), (128,), 8, 3873, jnp.int32)
        return (x, itok_B_8_3872)
    x, itok_B_8_3872 = _rec_inputs()

    def _L0_cond_setup():
        import math
        import jax, jax.numpy as jnp
        import numpy as np
        H, N, B, L = (32, 64, 16, 512)
        DT_MIN, DT_MAX = (0.001, 0.1)

        def _get_kernel(log_dt, C, log_A_real, A_imag, length):
            Cc = C[..., 0] + 1j * C[..., 1]
            dt = jnp.exp(log_dt)
            A = -jnp.exp(log_A_real) + 1j * A_imag
            dtA = A * dt[:, None]
            P = dtA[:, :, None] * jnp.arange(length, dtype=jnp.float32)
            Cs = Cc * (jnp.exp(dtA) - 1.0) / A
            K = 2.0 * jnp.einsum('hn,hnl->hl', Cs, jnp.exp(P)).real
            return K
        key = jax.random.key(seed)
        ks = jax.random.split(key, 6)
        u = jax.random.normal(ks[0], (B, H, L), dtype=jnp.float32)
        length = jax.random.randint(ks[1], (B,), 0, L)
        log_dt = jax.random.uniform(ks[2], (H,), dtype=jnp.float32) * (math.log(DT_MAX) - math.log(DT_MIN)) + math.log(DT_MIN)
        C = jax.random.normal(ks[3], (H, N, 2), dtype=jnp.float32)
        log_A_real = jnp.log(0.5 * jnp.ones((H, N), dtype=jnp.float32))
        A_imag = math.pi * jnp.broadcast_to(jnp.arange(N, dtype=jnp.float32), (H, N))
        D = jax.random.normal(ks[4], (H,), dtype=jnp.float32)
        return {'u': u, 'length': length, 'log_dt': log_dt, 'C': C, 'log_A_real': log_A_real, 'A_imag': A_imag, 'D': D}
    _L0_cond_all = _L0_cond_setup()
    _L0_cond_in = {k: v for k, v in _L0_cond_all.items() if k in ('log_dt', 'C', 'log_A_real', 'A_imag', 'D')}
    del _L0_cond_all

    def _L0_ffn_setup():
        import jax, jax.numpy as jnp
        import numpy as np
        IN_F = 512
        OUT_F = 512
        N_CLUSTERS = 64
        THRESHOLD = 0.01
        TEMPERATURE = 0.1
        BATCH, SEQ = (4, 256)
        key = jax.random.key(seed)
        k1, k2, k3, k4, k5 = jax.random.split(key, 5)
        s = 1.0 / np.sqrt(IN_F)
        return {'input': jax.random.normal(k1, (BATCH, SEQ, IN_F), dtype=jnp.float32), 'weight': jax.random.normal(k2, (OUT_F, IN_F), dtype=jnp.float32) * s, 'bias': jax.random.uniform(k3, (OUT_F,), dtype=jnp.float32, minval=-s, maxval=s), 'centroids': jax.random.normal(k4, (N_CLUSTERS, IN_F), dtype=jnp.float32) * s, 'assignments': jax.random.randint(k5, (OUT_F,), 0, N_CLUSTERS, dtype=jnp.int32)}
    _L0_ffn_all = _L0_ffn_setup()
    _L0_ffn_in = {k: v for k, v in _L0_ffn_all.items() if k in ('weight', 'bias', 'centroids', 'assignments')}
    del _L0_ffn_all
    return {'x': x, 'itok_B_8_3872': itok_B_8_3872, 'L0_cond_log_dt': _L0_cond_in['log_dt'], 'L0_cond_C': _L0_cond_in['C'], 'L0_cond_log_A_real': _L0_cond_in['log_A_real'], 'L0_cond_A_imag': _L0_cond_in['A_imag'], 'L0_cond_D': _L0_cond_in['D'], 'L0_ffn_weight': _L0_ffn_in['weight'], 'L0_ffn_bias': _L0_ffn_in['bias'], 'L0_ffn_centroids': _L0_ffn_in['centroids'], 'L0_ffn_assignments': _L0_ffn_in['assignments']}

def reference(x, itok_B_8_3872, L0_cond_log_dt, L0_cond_C, L0_cond_log_A_real, L0_cond_A_imag, L0_cond_D, L0_ffn_weight, L0_ffn_bias, L0_ffn_centroids, L0_ffn_assignments):
    import jax
    import jax.numpy as jnp

    def _L0_cond_ref(u, length, log_dt, C, log_A_real, A_imag, D):
        import math
        import jax, jax.numpy as jnp
        import numpy as np
        H, N, B, L = (32, 64, 16, 512)
        DT_MIN, DT_MAX = (0.001, 0.1)

        def _get_kernel(log_dt, C, log_A_real, A_imag, length):
            Cc = C[..., 0] + 1j * C[..., 1]
            dt = jnp.exp(log_dt)
            A = -jnp.exp(log_A_real) + 1j * A_imag
            dtA = A * dt[:, None]
            P = dtA[:, :, None] * jnp.arange(length, dtype=jnp.float32)
            Cs = Cc * (jnp.exp(dtA) - 1.0) / A
            K = 2.0 * jnp.einsum('hn,hnl->hl', Cs, jnp.exp(P)).real
            return K
        Bq, Hq, Lq = u.shape
        mask = (jnp.arange(Lq) < length[:, None]).astype(u.dtype)
        u_m = u * mask[:, None, :]
        kernel = _get_kernel(log_dt, C, log_A_real, A_imag, Lq)
        n = 2 * Lq
        k_f = jnp.fft.rfft(kernel, n=n)
        u_f = jnp.fft.rfft(u_m, n=n)
        y = jnp.fft.irfft(u_f * k_f, n=n)[..., :Lq]
        y = y + u_m * D[:, None]
        return y * mask[:, None, :]

    def _L0_ffn_ref(input, weight, bias, centroids, assignments):
        import jax, jax.numpy as jnp
        import numpy as np
        IN_F = 512
        OUT_F = 512
        N_CLUSTERS = 64
        THRESHOLD = 0.01
        TEMPERATURE = 0.1
        BATCH, SEQ = (4, 256)
        shape = input.shape
        x = input.reshape(-1, shape[-1])
        dots = jax.nn.softmax(x @ centroids.T / TEMPERATURE, axis=-1)
        hits = dots > THRESHOLD
        query_sel = jnp.any(hits, axis=1)
        cluster_sel = jnp.any(hits, axis=0)
        row_sel = cluster_sel[assignments]
        dense = x @ weight.T + bias
        out = jnp.where(query_sel[:, None] & row_sel[None, :], dense, jnp.zeros((), dense.dtype))
        return out.reshape(*shape[:-1], -1)
    x = x + _L0_ffn_ref(_L0_cond_ref(x, itok_B_8_3872, L0_cond_log_dt, L0_cond_C, L0_cond_log_A_real, L0_cond_A_imag, L0_cond_D), L0_ffn_weight, L0_ffn_bias, L0_ffn_centroids, L0_ffn_assignments)
    return x

_drawn_inputs = setup_inputs


def setup_inputs(seed=0):
    import zlib

    import numpy as np

    out = dict(_drawn_inputs(seed))
    spreads = {'L0_cond_log_A_real': (-0.6931471824645996, 0.2)}
    factors = {'L0_ffn_bias': 4.207}
    for name, (base, spread) in spreads.items():
        noise = np.random.default_rng([zlib.crc32(name.encode()), seed]).standard_normal(out[name].shape)
        drawn = base * np.exp(spread * noise) if base else spread * noise
        out[name] = jnp.asarray(drawn.astype(out[name].dtype))
    for name, factor in factors.items():
        out[name] = (out[name] * factor).astype(out[name].dtype)
    return out
```

```python
import math
from contextlib import ExitStack

import numpy as np
import concourse.bass as bass
from concourse import mybir

F32 = mybir.dt.float32
F32R = mybir.dt.float32r
BF16 = mybir.dt.bfloat16
I32 = mybir.dt.int32
ALU = mybir.AluOpType
ACT = mybir.ActivationFunctionType
AX = mybir.AxisListType

P = 128
H = 32
L = 512
J = L // P
N = 64
O = 512
NC = 64
LC = 32
LA = L // LC
LV = LC + LA
TAIL = P
KR = L + TAIL
G = 4
T = H // G
MAGIC = 1.5 * 2.0 ** 23
MAGIC_BITS_SHIFT = 23
TWO_PI = float(np.nextafter(np.float32(2 * math.pi), np.float32(0)))
LN2_HI = 0.693359375
LN2_LO = math.log(2.0) - LN2_HI
TEMPERATURE = 0.1
THRESHOLD = 0.01


def exp_coefficients(degree=6):
    n = degree
    nodes = np.cos((2 * np.arange(n) + 1) * np.pi / (2 * n)) * (math.log(2.0) / 2 * 1.02)
    a = np.vander(nodes, n, increasing=True)
    return [float(v) for v in np.linalg.solve(a, np.expm1(nodes) / nodes)]


def program(nc, x, lengths, log_dt, C, log_A_real, A_imag, D, weight, bias, centroids, assignments, out):
    ctx = ExitStack()
    with ctx:
        def sb(name, shape, dt=F32):
            return ctx.enter_context(nc.sbuf_tensor(name, shape, dt))

        def ps(name, shape, dt=F32):
            return ctx.enter_context(nc.psum_tensor(name, shape, dt))

        def sem(name):
            return ctx.enter_context(nc.semaphore(name))

        scratch = nc.dram_tensor("kernel_reversed", (2, H, KR), F32, kind="Internal").ap()

        y_all = sb("y_all", [P, H, J * P])
        used = [0]

        def early(parts, shape, dt=F32):
            n = int(np.prod(shape))
            piece = y_all[0:parts, :, :].rearrange("p h b -> p (h b)")[:, used[0]:used[0] + n]
            used[0] += n
            assert used[0] <= H * J * P
            if dt != F32:
                piece = piece.bitcast(dt)
            if len(shape) == 2:
                piece = piece.rearrange("p (a b) -> p a b", b=shape[1])
            return piece

        ident = sb("ident", [P, P])
        flip = sb("flip", [P, P])
        lval = sb("lval", [P, LV])
        pos = sb("pos", [P, J])
        clus = sb("clus", [NC, 1])
        zero = sb("zero", [2 * H, TAIL])
        half_pi = sb("half_pi", [P, 1])

        nat = sb("nat", [H, 2, P])
        cin = sb("cin", [H, N, 2])
        cnat = sb("cnat", [H, 2, P])
        d_at0 = sb("d_at0", [LA, H])
        len_i = early(P, (P,), I32)
        len_f = early(P, (P,))
        mask = sb("mask", [P, J, P])
        w_nat = sb("w_nat", [P, J, L])
        cen_nat = early(NC, (L,))
        wT = sb("wT", [P, J, O])
        cT = early(P, (J, NC))
        w_hi = sb("w_hi", [P, J, O], F32R)
        w_lo = sb("w_lo", [P, J, O], F32R)
        cenT = sb("cenT", [P, J, NC])
        bias_b = sb("bias_b", [P, O])
        asg_i = early(NC, (O,), I32)
        asg_f = early(NC, (O,))
        onehot = sb("onehot", [NC, O], BF16)

        ex = sb("ex", [P, 2, H])
        aim = sb("aim", [P, H])
        cc = sb("cc", [P, 2, H])
        tmp = [sb(f"tmp{i}", [P, 2, H]) for i in range(12)]
        dta_r = sb("dta_r", [P, H])
        turns = sb("turns", [P, H])
        s1 = sb("s1", [P, H])
        sh = sb("sh", [P, H])
        th = sb("th", [P, H])
        coef = sb("coef", [P, 2, H])
        phase = early(P, (H, LV))
        whole = early(P, (H, LV))
        absph = early(P, (H, LV))
        grow = early(P, (H, LV))
        osc = early(P, (H, LC))
        cos_a = early(P, (H, LA))
        sin_a = early(P, (H, LA))
        f_c = early(P, (H, LC))
        g_a = early(P, (H, LA))
        g_b = early(P, (H, LA))
        k_hi = early(LA, (H, LC), F32R)
        k_lo = early(LA, (H, LC), F32R)

        x_in = [sb(f"x_in{i}", [P, L]) for i in range(G)]
        toep = [sb(f"toep{i}", [P, 2, L], F32R) for i in range(G)]
        u_hi = [sb(f"u_hi{i}", [P, J * P], F32R) for i in range(2)]
        u_lo = [sb(f"u_lo{i}", [P, J * P], F32R) for i in range(2)]
        y_m = [sb(f"y_m{i}", [P, J * P]) for i in range(2)]
        y_hi = [sb(f"y_hi{i}", [P, J * P], F32R) for i in range(G)]
        y_lo = [sb(f"y_lo{i}", [P, J * P], F32R) for i in range(G)]
        dense = [sb(f"dense{i}", [P, O]) for i in range(G)]
        chosen = [sb(f"chosen{i}", [P, O]) for i in range(2)]
        result = [sb(f"result{i}", [P, O]) for i in range(G)]

        top = sb("top", [P, H])
        above = sb("above", [P, G, NC])
        e = sb("e", [P, G, NC])
        total = sb("total", [P, H])
        inv = sb("inv", [P, H])
        prob = sb("prob", [P, G, NC])
        best = sb("best", [P, G, NC])
        best1 = sb("best1", [P, NC])
        query = sb("query", [P, H])
        best_c = sb("best_c", [NC, 1])
        sel_b = sb("sel_b", [NC, P], BF16)
        rows = sb("rows", [P, O])

        spare = [ps(f"spare{i}", [P, 512]) for i in range(2)]
        ut = [ps(f"ut{i}", [P, 512]) for i in range(2)]
        yt = [ps(f"yt{i}", [P, 512]) for i in range(2)]
        lg = [ps(f"lg{i}", [P, 512]) for i in range(2)]
        wbank = [ut[0], ut[1], lg[0], lg[1]]
        bank = [spare[0], spare[1], ut[0], ut[1]]

        small_in = sem("small_in")
        dt_in = sem("dt_in")
        d_in = sem("d_in")
        w_in = sem("w_in")
        row_in = sem("row_in")
        tail_out = sem("tail_out")
        k_out = sem("k_out")
        x_arrived = [sem(f"x_arrived{i}") for i in range(G)]
        toep_arrived = [sem(f"toep_arrived{i}") for i in range(G)]
        stored = [sem(f"stored{i}") for i in range(G)]
        consts = sem("consts")
        pool_step = sem("pool_step")
        dve_step = sem("dve_step")
        act_step = sem("act_step")
        c_ready = sem("c_ready")
        params_t = sem("params_t")
        dta_ready = sem("dta_ready")
        phase_ready = sem("phase_ready")
        turn_ready = sem("turn_ready")
        sin_ready = sem("sin_ready")
        osc_ready = sem("osc_ready")
        grow_ready = sem("grow_ready")
        exp_ready = sem("exp_ready")
        tanh_ready = sem("tanh_ready")
        fg_ready = sem("fg_ready")
        k_ready = sem("k_ready")
        d_added = sem("d_added")
        k_hi_ready = sem("k_hi_ready")
        k_lo_ready = sem("k_lo_ready")
        wt_ready = sem("wt_ready")
        wt_copied = sem("wt_copied")
        wf_ready = sem("wf_ready")
        wf_hi = sem("wf_hi")
        wf_done = sem("wf_done")
        ut_ready = sem("ut_ready")
        u_hi_ready = sem("u_hi_ready")
        u_ready = sem("u_ready")
        conv_done = sem("conv_done")
        y_ready = sem("y_ready")
        y_kept = sem("y_kept")
        logits_done = sem("logits_done")
        above_ready = sem("above_ready")
        e_ready = sem("e_ready")
        inv_ready = sem("inv_ready")
        prob_ready = sem("prob_ready")
        best_t = sem("best_t")
        sel_ready = sem("sel_ready")
        rows_ps = sem("rows_ps")
        y_hi_ready = sem("y_hi_ready")
        y_split = sem("y_split")
        dense_done = sem("dense_done")
        dense_read = sem("dense_read")
        chosen_ready = sem("chosen_ready")
        result_ready = sem("result_ready")

        block = ctx.enter_context(nc.Block())

        def toep_source(h):
            src = scratch[:, h, 0:L]
            return bass.AP(src.tensor, src.offset, [[1, P], [H * KR, 2], [1, L]])

        @block.sync
        def _(sp):
            sp.dma_start(nat[:, 0, 0:N], log_A_real).then_inc(small_in, 16)
            sp.dma_start(nat[:, 0, N:P], log_A_real).then_inc(small_in, 16)
            sp.dma_start(nat[:, 1, 0:N], A_imag).then_inc(small_in, 16)
            sp.dma_start(nat[:, 1, N:P], A_imag).then_inc(small_in, 16)
            sp.dma_start(ex[:, 1, :], log_dt.rearrange("(a h) -> a h", a=1).to_broadcast((P, H))).then_inc(dt_in, 16)
            for s in range(G):
                sp.dma_start(x_in[s][:, :], x[:, s, :]).then_inc(x_arrived[s], 16)
            sp.wait_ge(consts, 6)
            sp.dma_start(scratch[:, :, L:KR].rearrange("a h t -> (a h) t"), zero[:, :]).then_inc(tail_out, 16)
            sp.wait_ge(k_hi_ready, 1)
            sp.dma_start(scratch[0, :, 0:L].rearrange("h (a c) -> a h c", a=LA), k_hi[:, :, :].bitcast(F32)).then_inc(k_out, 16)
            sp.wait_ge(k_lo_ready, 1)
            sp.dma_start(scratch[1, :, 0:L].rearrange("h (a c) -> a h c", a=LA), k_lo[:, :, :].bitcast(F32)).then_inc(k_out, 16)
            sp.wait_ge(tail_out, 16)
            sp.wait_ge(k_out, 32)
            for s in range(G):
                sp.dma_start(toep[s][:, :, :].bitcast(F32), toep_source(s)).then_inc(toep_arrived[s], 16)
            with sp.Fori(1, T) as t:
                for s in range(G):
                    h = t * G + s
                    sp.wait_ge(ut_ready, h - G + 1)
                    sp.dma_start(x_in[s][:, :], x[:, h, :]).then_inc(x_arrived[s], 16)
                    sp.wait_ge(conv_done, h - G + 1)
                    sp.dma_start(toep[s][:, :, :].bitcast(F32), toep_source(h)).then_inc(toep_arrived[s], 16)
            for s in range(G):
                sp.wait_ge(ut_ready, H - G + s + 1)
                sp.dma_start(x_in[s][:, :], x[:, s, :]).then_inc(x_arrived[s], 16)
            with sp.Fori(1, T) as t:
                for s in range(G):
                    h = t * G + s
                    sp.wait_ge(result_ready, h - G + 1)
                    sp.dma_start(out[:, h - G, :], result[s][:, :]).then_inc(stored[s], 16)
                    sp.dma_start(x_in[s][:, :], x[:, h, :]).then_inc(x_arrived[s], 16)
            for s in range(G):
                sp.wait_ge(result_ready, H - G + s + 1)
                sp.dma_start(out[:, H - G + s, :], result[s][:, :]).then_inc(stored[s], 16)
            for s in range(G):
                sp.wait_ge(stored[s], 16 * T)

        @block.gpsimd
        def _(pool):
            made = [0]

            def link(ins):
                made[0] += 1
                ins.then_inc(pool_step, 1)
                pool.wait_ge(pool_step, made[0])

            link(pool.memset(ident[:, :], 0.0))
            link(pool.memset(flip[:, :], 0.0))
            pool.affine_select(out=ident[:, :], in_=ident[:, :], compare_op=ALU.not_equal, fill=1.0, base=0,
                               pattern=[[-1, P]], channel_multiplier=1).then_inc(consts, 1)
            pool.iota(lval[:, 0:LC], [[-1, LC]], base=LC - 1, channel_multiplier=0,
                      allow_small_or_imprecise_dtypes=True).then_inc(consts, 1)
            pool.iota(lval[:, LC:LV], [[-LC, LA]], base=L - LC, channel_multiplier=0,
                      allow_small_or_imprecise_dtypes=True).then_inc(consts, 1)
            pool.memset(half_pi[:, :], math.pi / 2).then_inc(consts, 1)
            pool.affine_select(out=flip[:, :], in_=flip[:, :], compare_op=ALU.not_equal, fill=1.0, base=1 - P,
                               pattern=[[1, P]], channel_multiplier=1).then_inc(consts, 1)
            pool.memset(zero[:, :], 0.0).then_inc(consts, 1)
            pool.iota(pos[:, :], [[P, J]], base=P - 1, channel_multiplier=-1,
                      allow_small_or_imprecise_dtypes=True).then_inc(consts, 1)
            pool.iota(clus[:, :], [[0, 1]], base=0, channel_multiplier=1,
                      allow_small_or_imprecise_dtypes=True).then_inc(consts, 1)
            pool.memset(best[:, :, :], 0.0).then_inc(consts, 1)
            link(pool.memset(d_at0[:, :], 0.0))
            pool.dma_start(d_at0[LA - 1:LA, :], D.rearrange("(a h) -> a h", a=1)).then_inc(d_in, 16)
            pool.wait_ge(dta_ready, 1)
            pool.tensor_tensor(grow[:, :, :], dta_r[:, :].unsqueeze(2).to_broadcast((P, H, LV)),
                               lval[:, :].unsqueeze(1).to_broadcast((P, H, LV)), ALU.mult).then_inc(grow_ready, 1)

            with pool.Fori(0, T) as t:
                pool.wait_ge(inv_ready, t + 1)
                pool.tensor_tensor(prob[:, :, :], e[:, :, :],
                                   inv[:, bass.ds(t * G, G)].unsqueeze(2).to_broadcast((P, G, NC)),
                                   ALU.mult).then_inc(prob_ready, 1)

            def low_part(h, s):
                pool.wait_ge(y_hi_ready, h + 1)
                pool.tensor_tensor(y_lo[s][:, :], y_all[:, h, :], y_hi[s][:, :].bitcast(F32),
                                   ALU.subtract).then_inc(y_split, 1)

            def residual(t, s, h):
                pool.wait_ge(chosen_ready, h + 1)
                pool.wait_ge(x_arrived[s], 16 * (T + 1) + 16 * t)
                pool.wait_ge(stored[s], 16 * t)
                pool.tensor_tensor(result[s][:, :], chosen[s % 2][:, :], x_in[s][:, :], ALU.add).then_inc(result_ready, 1)

            AHEAD = 3
            for s in range(AHEAD):
                low_part(s, s)
            with pool.Fori(0, T - 1) as t:
                for s in range(G):
                    low_part(t * G + s + AHEAD, (s + AHEAD) % G)
                    residual(t, s, t * G + s)
            for s in range(G):
                if s + AHEAD < G:
                    low_part(H - G + s + AHEAD, s + AHEAD)
                residual(T - 1, s, H - G + s)

        @block.scalar
        def _(act):
            act.dma_start(cin[:, :, :], C).then_inc(small_in, 16)
            act.dma_start(w_nat[:, :, :], weight.rearrange("(j p) l -> p j l", p=P)).then_inc(w_in, 16)
            act.dma_start(cen_nat[:, :], centroids).then_inc(w_in, 16)
            act.dma_start(len_i[:, :], lengths.rearrange("(a b) -> a b", a=1).to_broadcast((P, P))).then_inc(row_in, 16)
            act.dma_start(bias_b[:, :], bias.rearrange("(a o) -> a o", a=1).to_broadcast((P, O))).then_inc(row_in, 16)
            act.dma_start(asg_i[:, :], assignments.rearrange("(a o) -> a o", a=1).to_broadcast((NC, O))).then_inc(row_in, 16)
            act.wait_ge(turn_ready, 1)
            act.activation(s1[:, :], tmp[11][:, 0, :], ACT.Sin, scale=TWO_PI).then_inc(sin_ready, 1)
            act.activation(sh[:, :], tmp[11][:, 0, :], ACT.Sin, scale=TWO_PI / 2).then_inc(sin_ready, 1)
            act.wait_ge(phase_ready, 2)
            act.wait_ge(consts, 4)
            act.activation(cos_a[:, :, :], absph[:, :, LC:LV], ACT.Sin, scale=-TWO_PI, bias=half_pi[:, :]).then_inc(osc_ready, 1)
            act.activation(sin_a[:, :, :], phase[:, :, LC:LV], ACT.Sin, scale=TWO_PI).then_inc(osc_ready, 1)
            act.activation(osc[0:N, :, :], absph[0:N, :, 0:LC], ACT.Sin, scale=-TWO_PI, bias=half_pi[0:N, :]).then_inc(osc_ready, 1)
            act.activation(osc[N:P, :, :], phase[N:P, :, 0:LC], ACT.Sin, scale=TWO_PI).then_inc(osc_ready, 1)
            act.activation(th[:, :], dta_r[:, :], ACT.Tanh, scale=0.5).then_inc(tanh_ready, 1)
            act.wait_ge(grow_ready, 1)
            act.activation(whole[:, :, :], grow[:, :, :], ACT.Exp).then_inc(exp_ready, 1)
            act.wait_ge(wt_ready, 1)
            for j in range(J):
                act.activation(wT[:, j, :], wbank[j][:, :], ACT.Copy).then_inc(wt_copied, 1)
            act.activation(cT[:, :, :], yt[1][:, 0:J * NC].rearrange("p (j c) -> p j c", c=NC), ACT.Copy).then_inc(wt_copied, 1)
            act.wait_ge(d_added, 1)
            for b in range(2):
                last = act.activation(k_hi[:, 16 * b:16 * b + 16, :], spare[b][0:LA, :].rearrange("a (h c) -> a h c", c=LC), ACT.Copy)
            last.then_inc(k_hi_ready, 1)
            act.wait_ge(wf_ready, 1)
            act.activation(cenT[:, :, :], yt[1][:, 0:J * NC].rearrange("p (j c) -> p j c", c=NC), ACT.Copy).then_inc(wf_done, 1)
            for j in range(J):
                act.wait_ge(wf_ready, j + 2)
                act.activation(w_hi[:, j, :], wbank[j][:, :], ACT.Copy).then_inc(wf_hi, 1)

            def high_u(h, s, first=False):
                act.wait_ge(ut_ready, h + 1)
                if not first:
                    act.wait_ge(conv_done, h - 1)
                act.activation(u_hi[s % 2][:, :], ut[s % 2][:, :], ACT.Copy).then_inc(u_hi_ready, 1)

            def keep_y(h, s):
                act.wait_ge(y_ready, h + 1)
                act.activation(y_all[:, h, :], y_m[s % 2][:, :], ACT.Copy).then_inc(y_kept, 1)

            def exps(t):
                act.wait_ge(above_ready, t + 1)
                act.wait_ge(prob_ready, t)
                act.activation(e[:, :, :], above[:, :, :], ACT.Exp, scale=1.0 / TEMPERATURE).then_inc(e_ready, 1)

            high_u(0, 0, True)
            for s in range(G):
                high_u(s + 1, s + 1, s < 1)
                keep_y(s, s)
            with act.Fori(1, T - 1) as t:
                for s in range(G):
                    high_u(t * G + s + 1, s + 1)
                    keep_y(t * G + s, s)
                    if s == 1:
                        exps(t - 1)
            for s in range(G):
                if s < G - 1:
                    high_u(H - G + s + 1, s + 1)
                keep_y(H - G + s, s)
                if s == 1:
                    exps(T - 2)
            exps(T - 1)

            def high_y(h, s, first=False):
                if not first:
                    act.wait_ge(dense_done, h - G + 1)
                act.activation(y_hi[s][:, :], y_all[:, h, :], ACT.Copy).then_inc(y_hi_ready, 1)

            act.wait_ge(y_kept, H)
            for s in range(G):
                high_y(s, s, True)
            with act.Fori(1, T) as t:
                for s in range(G):
                    high_y(t * G + s, s)

        @block.vector
        def _(dve):
            made = [0]

            def link(ins):
                made[0] += 1
                ins.then_inc(dve_step, 1)
                dve.wait_ge(dve_step, made[0])

            tt, ts, stt = nc.vector.tensor_tensor, nc.vector.tensor_scalar, nc.vector.scalar_tensor_tensor
            dve.wait_ge(small_in, 16 * 5)
            ts(cnat[:, 0, 0:N], cin[:, :, 0], 2.0, None, ALU.mult)
            ts(cnat[:, 0, N:P], cin[:, :, 1], -2.0, None, ALU.mult)
            ts(cnat[:, 1, 0:N], cin[:, :, 1], 2.0, None, ALU.mult)
            ts(cnat[:, 1, N:P], cin[:, :, 0], 2.0, None, ALU.mult).then_inc(c_ready, 1)
            dve.wait_ge(params_t, 1)
            tt_ps = yt[0][:, 0:4 * H].rearrange("p (k h) -> p k h", h=H)
            nc.vector.tensor_copy(ex[:, 0, :], tt_ps[:, 0, :])
            nc.vector.tensor_copy(aim[:, :], tt_ps[:, 1, :])
            link(nc.vector.tensor_copy(cc[:, :, :], tt_ps[:, 2:4, :]))
            dve.wait_ge(dt_in, 16)
            v = ex[:, :, :]
            kf, k, r, q = (tmp[i][:, :, :] for i in range(4))
            c = exp_coefficients()
            link(ts(v, v, -87.0, 88.0, ALU.max, ALU.min))
            link(ts(kf, v, 1.0 / math.log(2.0), MAGIC, ALU.mult, ALU.add))
            link(ts(k, kf, MAGIC, None, ALU.subtract))
            link(stt(r, k, -LN2_HI, v, ALU.mult, ALU.add))
            link(stt(r, k, -LN2_LO, r, ALU.mult, ALU.add))
            ki = tmp[4][:, :, :].bitcast(I32)
            ts(ki, kf.bitcast(I32), MAGIC_BITS_SHIFT, None, ALU.logical_shift_left)
            link(ts(q, r, c[-1], None, ALU.mult))
            for cj in c[-2::-1]:
                link(stt(q, q, cj, r, ALU.add, ALU.mult))
            link(ts(q, q, 1.0, None, ALU.add))
            link(tt(v.bitcast(I32), q.bitcast(I32), ki, ALU.add))
            e_re, dt = ex[:, 0, :], ex[:, 1, :]
            stt(dta_r[:, :], e_re, -1.0, dt, ALU.mult, ALU.mult).then_inc(dta_ready, 1)
            link(tt(tmp[10][:, 0, :], aim[:, :], dt, ALU.mult))
            link(ts(turns[:, :], tmp[10][:, 0, :], 1.0 / (2 * math.pi), None, ALU.mult))
            link(ts(tmp[10][:, 1, :], turns[:, :], MAGIC, MAGIC, ALU.add, ALU.subtract))
            tt(tmp[11][:, 0, :], turns[:, :], tmp[10][:, 1, :], ALU.subtract).then_inc(turn_ready, 1)
            dve.wait_ge(consts, 3)
            link(tt(phase[:, :, :], turns[:, :].unsqueeze(2).to_broadcast((P, H, LV)),
                    lval[:, :].unsqueeze(1).to_broadcast((P, H, LV)), ALU.mult))
            link(ts(whole[:, :, :], phase[:, :, :], MAGIC, MAGIC, ALU.add, ALU.subtract))
            tt(phase[:, :, :], phase[:, :, :], whole[:, :, :], ALU.subtract).then_inc(phase_ready, 1)
            dve.wait_ge(phase_ready, 1)
            ts(absph[:, :, :].bitcast(I32), phase[:, :, :].bitcast(I32), 0x7FFFFFFF, None, ALU.bitwise_and).then_inc(phase_ready, 1)
            a = aim[:, :]
            T1, T2, T3, T4, T5, T6, T7, T8 = (tmp[i][:, 0, :] for i in range(8))
            link(stt(T1, e_re, 1.0, e_re, ALU.mult, ALU.mult))
            link(tt(T2, a, a, ALU.mult))
            link(tt(T1, T1, T2, ALU.add))
            link(nc.vector.reciprocal(T1, T1))
            dve.wait_ge(sin_ready, 2)
            link(stt(T2, sh[:, :], -2.0, sh[:, :], ALU.mult, ALU.mult))
            dve.wait_ge(tanh_ready, 1)
            link(ts(T3, th[:, :], -1.0, 1.0, ALU.mult, ALU.add))
            link(nc.vector.reciprocal(T3, T3))
            link(stt(T3, th[:, :], 2.0, T3, ALU.mult, ALU.mult))
            link(stt(T4, T2, 1.0, T3, ALU.add, ALU.mult))
            link(tt(T4, T4, T2, ALU.add))
            link(stt(T5, T3, 1.0, s1[:, :], ALU.add, ALU.mult))
            link(tt(T6, T5, a, ALU.mult))
            link(tt(T7, T4, e_re, ALU.mult))
            link(tt(T6, T6, T7, ALU.subtract))
            link(tt(T6, T6, T1, ALU.mult))
            link(tt(T7, T4, a, ALU.mult))
            link(tt(T8, T5, e_re, ALU.mult))
            link(tt(T7, T7, T8, ALU.add))
            link(stt(T7, T7, -1.0, T1, ALU.mult, ALU.mult))
            link(tt(T1, cc[:, 0, :], T6, ALU.mult))
            link(tt(T2, cc[:, 1, :], T7, ALU.mult))
            tt(coef[:, 0, :], T1, T2, ALU.subtract)
            link(tt(T3, cc[:, 0, :], T7, ALU.mult))
            link(tt(T4, cc[:, 1, :], T6, ALU.mult))
            link(stt(coef[:, 1, :], T3, -1.0, T4, ALU.mult, ALU.subtract))
            dve.wait_ge(osc_ready, 4)
            tt(g_a[:, :, :], cos_a[:, :, :], coef[:, 0, :].unsqueeze(2).to_broadcast((P, H, LA)), ALU.mult)
            link(tt(g_b[:, :, :], sin_a[:, :, :], coef[:, 1, :].unsqueeze(2).to_broadcast((P, H, LA)), ALU.mult))
            link(tt(g_a[:, :, :], g_a[:, :, :], g_b[:, :, :], ALU.add))
            dve.wait_ge(exp_ready, 1)
            tt(g_a[:, :, :], g_a[:, :, :], whole[:, :, LC:LV], ALU.mult)
            tt(f_c[:, :, :], osc[:, :, :], whole[:, :, 0:LC], ALU.mult).then_inc(fg_ready, 1)
            dve.wait_ge(k_ready, 1)
            dve.wait_ge(d_in, 16)
            for b in range(2):
                at0 = spare[b][0:LA, :].rearrange("a (h c) -> a h c", c=LC)[:, :, LC - 1]
                last = tt(at0, at0, d_at0[:, 16 * b:16 * b + 16], ALU.add)
            last.then_inc(d_added, 1)
            dve.wait_ge(k_hi_ready, 1)
            for b in range(2):
                last = tt(k_lo[:, 16 * b:16 * b + 16, :], spare[b][0:LA, :].rearrange("a (h c) -> a h c", c=LC),
                          k_hi[:, 16 * b:16 * b + 16, :].bitcast(F32), ALU.subtract)
            last.then_inc(k_lo_ready, 1)
            dve.wait_ge(row_in, 48)
            dve.wait_ge(consts, 9)
            nc.vector.tensor_copy(len_f[:, :], len_i[:, :])
            link(nc.vector.tensor_copy(asg_f[:, :], asg_i[:, :]))
            for j in range(J):
                ts(mask[:, j, :], len_f[:, :], pos[:, j:j + 1], None, ALU.is_gt)
            link(ts(onehot[:, :], asg_f[:, :], clus[:, :], None, ALU.is_equal))
            for j in range(J):
                dve.wait_ge(wf_hi, j + 1)
                tt(w_lo[:, j, :], wbank[j][:, :], w_hi[:, j, :].bitcast(F32), ALU.subtract).then_inc(wf_done, 1)
            mask_f = mask[:, :, :].rearrange("p j b -> p (j b)")

            def low_u(h, s):
                dve.wait_ge(u_hi_ready, h + 1)
                tt(u_lo[s % 2][:, :], ut[s % 2][:, :], u_hi[s % 2][:, :].bitcast(F32), ALU.subtract).then_inc(u_ready, 1)

            def mask_y(h, s, first=False):
                dve.wait_ge(conv_done, h + 1)
                if not first:
                    dve.wait_ge(logits_done, h - 1)
                    dve.wait_ge(y_kept, h - 1)
                tt(y_m[s % 2][:, :], yt[s % 2][:, :], mask_f, ALU.mult).then_inc(y_ready, 1)

            logits_ps = lg[0][:, 0:G * NC].rearrange("p (g c) -> p g c", c=NC)

            def softmax_top(t, hs):
                dve.wait_ge(logits_done, (t + 1) * G)
                nc.vector.reduce_max(top[:, hs], logits_ps, AX.X).then_inc(dve_step, 1)

            def softmax_above(t, hs, steps):
                dve.wait_ge(dve_step, steps)
                tt(above[:, :, :], logits_ps, top[:, hs].unsqueeze(2).to_broadcast((P, G, NC)),
                   ALU.subtract).then_inc(above_ready, 1)

            def softmax_sum(t, hs, steps):
                dve.wait_ge(e_ready, t + 1)
                nc.vector.reduce_sum(total[:, hs], e[:, :, :], AX.X).then_inc(dve_step, 1)
                dve.wait_ge(dve_step, steps)
                nc.vector.reciprocal(inv[:, hs], total[:, hs]).then_inc(inv_ready, 1)

            def softmax_best(t, steps):
                dve.wait_ge(prob_ready, t + 1)
                dve.wait_ge(dve_step, steps)
                tt(best[:, :, :], best[:, :, :], prob[:, :, :], ALU.max).then_inc(dve_step, 1)

            base = made[0]

            def softmax_part(s, t, hs, steps):
                if s == 0:
                    softmax_top(t, hs)
                    softmax_above(t, hs, steps + 1)
                if s == 2:
                    softmax_sum(t, hs, steps + 2)
                if s == 3:
                    softmax_best(t, steps)

            low_u(0, 0)
            for s in range(G):
                low_u(s + 1, s + 1)
                mask_y(s, s, s < 2)
            with dve.Fori(1, T - 1) as t:
                for s in range(G):
                    low_u(t * G + s + 1, s + 1)
                    mask_y(t * G + s, s)
                    softmax_part(s, t - 1, bass.ds(t * G - G, G), base + 3 * t - 3)
            for s in range(G):
                if s < G - 1:
                    low_u(H - G + s + 1, s + 1)
                mask_y(H - G + s, s)
                softmax_part(s, T - 2, slice(H - 2 * G, H - G), base + 3 * (T - 2))
            for s in range(G):
                softmax_part(s, T - 1, slice(H - G, H), base + 3 * (T - 1))
            made[0] = base + 3 * T
            dve.wait_ge(dve_step, made[0])
            dve.wait_ge(inv_ready, T)
            link(ts(query[:, :], inv[:, :], THRESHOLD, None, ALU.is_gt))
            nc.vector.reduce_max(best1[:, :], best[:, :, :].rearrange("p g c -> p c g"), AX.X).then_inc(sel_ready, 1)
            dve.wait_ge(best_t, 1)
            link(nc.vector.reduce_max(best_c[:, :], yt[0][0:NC, 0:P], AX.X))
            ts(sel_b[:, :], best_c[:, :].to_broadcast((NC, P)), THRESHOLD, None, ALU.is_gt).then_inc(sel_ready, 1)
            dve.wait_ge(rows_ps, 1)
            link(nc.vector.tensor_copy(rows[:, :], yt[1][:, :]))

            def add_bias(h, s, first=False):
                dve.wait_ge(dense_done, h + 1)
                if not first:
                    dve.wait_ge(chosen_ready, h - G + 1)
                tt(dense[s][:, :], bank[s][:, :], bias_b[:, :], ALU.add).then_inc(dense_read, 1)

            def choose(h, s, first=False):
                dve.wait_ge(dense_read, h + 1)
                if not first:
                    dve.wait_ge(result_ready, h - 1)
                q = query[:, bass.ds(h, 1)]
                stt(chosen[s % 2][:, :], dense[s][:, :], q, rows[:, :], ALU.mult, ALU.mult).then_inc(chosen_ready, 1)

            add_bias(0, 0, True)
            for s in range(G):
                add_bias(s + 1, (s + 1) % G, s < G - 1)
                choose(s, s, s < 2)
            with dve.Fori(1, T - 1) as t:
                for s in range(G):
                    add_bias(t * G + s + 1, (s + 1) % G)
                    choose(t * G + s, s)
            for s in range(G):
                if s < G - 1:
                    add_bias(H - G + s + 1, s + 1)
                choose(H - G + s, s)

        @block.tensor
        def _(pe):
            mm, tr = nc.tensor.matmul, nc.tensor.transpose
            pe.wait_ge(consts, 1)
            pe.wait_ge(c_ready, 1)
            for i, src in enumerate((nat[:, 0, :], nat[:, 1, :], cnat[:, 0, :], cnat[:, 1, :])):
                last = tr(yt[0][:, i * H:(i + 1) * H], src, ident[0:H, 0:H])
            last.then_inc(params_t, 1)
            pe.wait_ge(w_in, 32)
            pe.wait_ge(consts, 5)
            for j in range(J):
                for o in range(O // P):
                    tr(wbank[j][:, o * P:(o + 1) * P], w_nat[:, o, j * P:(j + 1) * P], ident[:, :])
                last = tr(yt[1][:, j * NC:(j + 1) * NC], cen_nat[:, j * P:(j + 1) * P], ident[0:NC, 0:NC])
            last.then_inc(wt_ready, 1)
            pe.wait_ge(fg_ready, 1)
            for h in range(H):
                last = mm(spare[h // 16][0:LA, (h % 16) * LC:(h % 16 + 1) * LC], g_a[:, h, :], f_c[:, h, :],
                          start=True, stop=True)
            last.then_inc(k_ready, 1)
            pe.wait_ge(wt_copied, J + 1)
            for j in range(J):
                last = mm(yt[1][:, j * NC:(j + 1) * NC], flip[:, :], cT[:, j, :], start=True, stop=True)
            last.then_inc(wf_ready, 1)
            for j in range(J):
                mm(wbank[j][:, :], flip[:, :], wT[:, j, :], start=True, stop=True).then_inc(wf_ready, 1)

            def transposes(t, s, h, first=False):
                pe.wait_ge(x_arrived[s], 16 * (t + 1))
                if not first:
                    pe.wait_ge(u_ready, h - 1)
                for j in range(J):
                    last = tr(ut[s % 2][:, j * P:(j + 1) * P], x_in[s][:, j * P:(j + 1) * P], ident[:, :])
                last.then_inc(ut_ready, 1)

            def convolution(t, s, h, first=False):
                pe.wait_ge(u_ready, h + 1)
                pe.wait_ge(toep_arrived[s], 16 * (t + 1))
                if not first:
                    pe.wait_ge(y_ready, h - 1)
                parts = ((0, u_hi), (0, u_lo), (1, u_hi))
                for d in range(J):
                    for i, (part, u) in enumerate(parts):
                        last = mm(yt[s % 2][:, d * P:], toep[s][:, part, (J - 1 - d) * P:(J - d) * P],
                                  u[s % 2][:, 0:(J - d) * P], start=(d == 0 and i == 0), stop=(d == J - 1 and i == 2))
                last.then_inc(conv_done, 1)

            def logits(s, h):
                pe.wait_ge(y_ready, h + 1)
                for j in range(J):
                    last = mm(lg[0][:, s * NC:(s + 1) * NC], y_m[s % 2][:, j * P:(j + 1) * P], cenT[:, j, :],
                              start=(j == 0), stop=(j == J - 1))
                last.then_inc(logits_done, 1)

            pe.wait_ge(wf_done, J + 1)
            transposes(0, 0, 0, True)
            for s in range(G):
                if s < G - 1:
                    transposes(0, s + 1, s + 1, s < 1)
                else:
                    transposes(1, 0, G)
                convolution(0, s, s, s < 2)
                if s > 0:
                    logits(s - 1, s - 1)
            with pe.Fori(1, T - 1) as t:
                for s in range(G):
                    h = t * G + s
                    transposes(t if s < G - 1 else t + 1, (s + 1) % G, h + 1)
                    convolution(t, s, h)
                    if s == 1:
                        pe.wait_ge(above_ready, t)
                    logits((s - 1) % G, h - 1)
            for s in range(G):
                h = H - G + s
                if s < G - 1:
                    transposes(T - 1, s + 1, h + 1)
                convolution(T - 1, s, h)
                if s == 1:
                    pe.wait_ge(above_ready, T - 1)
                logits((s - 1) % G, h - 1)
            logits(G - 1, H - 1)

            def layer(h, s, first=False):
                pe.wait_ge(y_split, h + 1)
                if not first:
                    pe.wait_ge(dense_read, h - G + 1)
                for j in range(J):
                    js = slice(j * P, (j + 1) * P)
                    mm(bank[s][:, :], y_hi[s][:, js], w_hi[:, j, :], start=(j == 0), stop=False)
                    mm(bank[s][:, :], y_hi[s][:, js], w_lo[:, j, :], start=False, stop=False)
                    last = mm(bank[s][:, :], y_lo[s][:, js], w_hi[:, j, :], start=False, stop=(j == J - 1))
                last.then_inc(dense_done, 1)

            layer(0, 0, True)
            layer(1, 1, True)
            pe.wait_ge(sel_ready, 1)
            tr(yt[0][0:NC, 0:P], best1[:, :], ident[:, :]).then_inc(best_t, 1)
            layer(2, 2, True)
            pe.wait_ge(sel_ready, 2)
            mm(yt[1][:, :], sel_b[:, :], onehot[:, :], start=True, stop=True).then_inc(rows_ps, 1)
            layer(3, 3, True)
            with pe.Fori(1, T) as t:
                for s in range(G):
                    layer(t * G + s, s)


_INS = ["x", "itok_B_8_3872", "L0_cond_log_dt", "L0_cond_C", "L0_cond_log_A_real", "L0_cond_A_imag", "L0_cond_D",
        "L0_ffn_weight", "L0_ffn_bias", "L0_ffn_centroids", "L0_ffn_assignments"]


def kernel(**inputs):
    import numpy as _np
    import concourse.bacc as _bacc
    from concourse import mybir as _mybir
    from concourse.bass_utils import run_bass_kernel_spmd as _run

    nc = _bacc.Bacc("TRN2", target_bir_lowering=False, num_devices=1)
    arrays, args = {}, []
    for name in _INS:
        a = _np.ascontiguousarray(inputs[name])
        arrays[f"in_{name}"] = a
        args.append(nc.dram_tensor(f"in_{name}", a.shape, _mybir.dt.from_np(a.dtype), kind="ExternalInput").ap())
    out = nc.dram_tensor("out_0", (P, H, L), _mybir.dt.float32, kind="ExternalOutput").ap()
    program(nc, *args, out)
    r = _run(nc, [arrays], core_ids=[0])
    return r.results[0]["out_0"]
```

```python
import math
from contextlib import ExitStack

import numpy as np
import concourse.bass as bass
from concourse import mybir

F32 = mybir.dt.float32
F32R = mybir.dt.float32r
BF16 = mybir.dt.bfloat16
I32 = mybir.dt.int32
ALU = mybir.AluOpType
ACT = mybir.ActivationFunctionType
AX = mybir.AxisListType

P = 128
H = 32
L = 512
J = L // P
N = 64
O = 512
NC = 64
LC = 32
LA = L // LC
LV = LC + LA
XS = 4
EARLY = 24
HH = H // 2
TAIL = P
KR = L + TAIL
G = 4
T = H // G
MAGIC = 1.5 * 2.0 ** 23
MAGIC_BITS_SHIFT = 23
TWO_PI = float(np.nextafter(np.float32(2 * math.pi), np.float32(0)))
LN2_HI = 0.693359375
LN2_LO = math.log(2.0) - LN2_HI
TEMPERATURE = 0.1
THRESHOLD = 0.01


def exp_coefficients(degree=6):
    n = degree
    nodes = np.cos((2 * np.arange(n) + 1) * np.pi / (2 * n)) * (math.log(2.0) / 2 * 1.02)
    a = np.vander(nodes, n, increasing=True)
    return [float(v) for v in np.linalg.solve(a, np.expm1(nodes) / nodes)]


def program(nc, x, lengths, log_dt, C, log_A_real, A_imag, D, weight, bias, centroids, assignments, out):
    ctx = ExitStack()
    with ctx:
        def sb(name, shape, dt=F32):
            return ctx.enter_context(nc.sbuf_tensor(name, shape, dt))

        def ps(name, shape, dt=F32):
            return ctx.enter_context(nc.psum_tensor(name, shape, dt))

        def sem(name):
            return ctx.enter_context(nc.semaphore(name))

        scratch = nc.dram_tensor("kernel_reversed", (H, KR), F32, kind="Internal").ap()

        WORK = 8192
        work = sb("work", [P, WORK])

        def carve(start, parts, shape):
            n = int(np.prod(shape))
            assert start + n <= WORK
            piece = work[0:parts, start:start + n]
            if len(shape) == 2:
                piece = piece.rearrange("p (a b) -> p a b", b=shape[1])
            if len(shape) == 3:
                piece = piece.rearrange("p (a b c) -> p a b c", b=shape[1], c=shape[2])
            return piece, start + n

        phase, at = carve(0, P, (HH, LV))
        whole, at = carve(at, P, (HH, LV))
        absph, at = carve(at, P, (HH, LV))
        grow, at = carve(at, P, (HH, LV))
        mag, at = carve(at, P, (HH, LV))
        osc, at = carve(at, P, (2, HH, LV))
        f_c, at = carve(at, P, (2, HH, LC))
        e_a, _ = carve(0, P, (2, HH, LA))
        e_p, _ = carve(HH * LV, P, (2, HH, LA))
        e_q, _ = carve(2 * HH * LV, P, (2, HH, LA))
        g_a, at = carve(at, P, (2, HH, LA))
        k_sb, at = carve(at, 2 * LA, (2, 512))
        w_nat, at = carve(0, P, (J, L))
        w_rev, at = carve(at, P, (J, L))
        chosen, at = [], 0
        dense, result = [], []
        for i in range(G):
            piece, at = carve(at, P, (O,))
            dense.append(piece)
        for i in range(2):
            piece, at = carve(at, P, (2, O))
            result.append(piece)
        for i in range(2):
            piece, at = carve(at, P, (O,))
            chosen.append(piece)

        ident = sb("ident", [P, P])
        lval = sb("lval", [P, LV])
        pos = sb("pos", [P, J])
        clus = sb("clus", [NC, 1])
        zero = sb("zero", [H, TAIL])
        half_pi = sb("half_pi", [P, 1])

        lar_n = sb("lar_n", [HH, 2, N])
        aim_n = sb("aim_n", [HH, 2, N])
        c_n = sb("c_n", [HH, 2, N, 2])
        d_at0 = sb("d_at0", [2 * LA, H])
        len_i = sb("len_i", [P, P], I32)
        len_f = sb("len_f", [P, P])
        mask = sb("mask", [P, J, P])
        w_hi = sb("w_hi", [P, J, O], F32R)
        w_lo = sb("w_lo", [P, J, O], F32R)
        cenT = sb("cenT", [P, J, NC])
        bias_b = sb("bias_b", [P, O])
        asg_i = sb("asg_i", [NC, O], I32)
        asg_f = sb("asg_f", [NC, O])
        onehot = sb("onehot", [NC, O], BF16)

        ex = sb("ex", [P, 2, HH])
        par = sb("par", [P, 3, HH])
        tmp = [sb(f"tmp{i}", [P, 2, HH]) for i in range(6)]
        abs2 = sb("abs2", [P, 2, HH])
        dta_r = sb("dta_r", [P, HH])
        turns = sb("turns", [P, HH])
        frac = sb("frac", [P, HH])
        s1 = sb("s1", [P, HH])
        sh = sb("sh", [P, HH])
        th = sb("th", [P, HH])
        coef = sb("coef", [P, 2, HH])

        x_in = [sb(f"x_in{i}", [P, 2, L]) for i in range(XS)]
        xy = sb("xy", [P, H, J * P])
        toep = [sb(f"toep{i}", [P, L]) for i in range(G)]
        t_hi = [sb(f"t_hi{i}", [P, L], F32R) for i in range(G)]
        t_lo = [sb(f"t_lo{i}", [P, L], F32R) for i in range(G)]
        u_hi = [sb(f"u_hi{i}", [P, J * P], F32R) for i in range(2)]
        u_lo = [sb(f"u_lo{i}", [P, J * P], F32R) for i in range(2)]
        y_m = [sb(f"y_m{i}", [P, J * P]) for i in range(2)]
        cen_nat, cen_rev = (y_m[i][0:NC, :] for i in range(2))
        y_hi = [sb(f"y_hi{i}", [P, J * P], F32R) for i in range(G)]
        y_lo = [sb(f"y_lo{i}", [P, J * P], F32R) for i in range(G)]

        top = sb("top", [P, H])
        above = sb("above", [P, G, NC])
        e = sb("e", [P, G, NC])
        total = sb("total", [P, H])
        inv = sb("inv", [P, H])
        prob = sb("prob", [P, G, NC])
        best = sb("best", [P, G, NC])
        best1 = sb("best1", [P, NC])
        query = sb("query", [P, H])
        best_c = sb("best_c", [NC, 1])
        sel_b = sb("sel_b", [NC, P], BF16)
        rows = sb("rows", [P, O])

        spare = [ps(f"spare{i}", [P, 512]) for i in range(2)]
        ut = [ps(f"ut{i}", [P, 512]) for i in range(2)]
        yt = [ps(f"yt{i}", [P, 512]) for i in range(2)]
        lg = [ps(f"lg{i}", [P, 512]) for i in range(2)]
        xt = [ut[0], ut[1], lg[0], lg[1]]
        bank = [spare[0], spare[1], ut[0], ut[1]]

        par_in = sem("par_in")
        dt_in = sem("dt_in")
        d_in = sem("d_in")
        w_in = sem("w_in")
        cen_in = sem("cen_in")
        len_in = sem("len_in")
        row_in = sem("row_in")
        tail_out = sem("tail_out")
        k_out = sem("k_out")
        x_arrived = [sem(f"x_arrived{i}") for i in range(XS)]
        x_back = [sem(f"x_back{i}") for i in range(2)]
        bias_in = sem("bias_in")
        toep_arrived = [sem(f"toep_arrived{i}") for i in range(G)]
        stored = [sem(f"stored{i}") for i in range(2)]
        consts = sem("consts")
        pool_step = sem("pool_step")
        dve_step = sem("dve_step")
        params_t = sem("params_t")
        dta_ready = sem("dta_ready")
        phase_ready = sem("phase_ready")
        turn_ready = sem("turn_ready")
        small_ready = sem("small_ready")
        osc_ready = sem("osc_ready")
        grow_ready = sem("grow_ready")
        mag_ready = sem("mag_ready")
        f_ready = sem("f_ready")
        g_ready = sem("g_ready")
        k_ready = sem("k_ready")
        d_added = sem("d_added")
        k_copied = sem("k_copied")
        rev_ready = sem("rev_ready")
        w_rev_ready = sem("w_rev_ready")
        wt_ready = sem("wt_ready")
        cen_copied = sem("cen_copied")
        w_hi_ready = sem("w_hi_ready")
        w_lo_ready = sem("w_lo_ready")
        ut_ready = sem("ut_ready")
        mask_ready = sem("mask_ready")
        asg_ready = sem("asg_ready")
        ut_kept = [sem(f"ut_kept{i}") for i in range(G)]
        t_hi_ready = sem("t_hi_ready")
        t_ready = sem("t_ready")
        u_hi_ready = sem("u_hi_ready")
        u_ready = sem("u_ready")
        conv_done = sem("conv_done")
        y_ready = sem("y_ready")
        y_kept = sem("y_kept")
        logits_done = sem("logits_done")
        above_ready = sem("above_ready")
        e_ready = sem("e_ready")
        inv_ready = sem("inv_ready")
        prob_ready = sem("prob_ready")
        best_ready = sem("best_ready")
        best_t = sem("best_t")
        sel_ready = sem("sel_ready")
        rows_ps = sem("rows_ps")
        y_hi_ready = sem("y_hi_ready")
        y_split = sem("y_split")
        dense_done = sem("dense_done")
        dense_read = sem("dense_read")
        chosen_ready = sem("chosen_ready")
        result_ready = sem("result_ready")

        def back(j):
            return slice((j + 1) * P - 1, j * P - 1 if j > 0 else None, -1)

        block = ctx.enter_context(nc.Block())

        def toep_source(h):
            src = scratch[h, 0:L]
            return bass.AP(src.tensor, src.offset, [[1, P], [1, L]])

        @block.sync
        def _(sp):
            sp.dma_start(lar_n[:, :, :], log_A_real.rearrange("(a h) n -> h a n", a=2)).then_inc(par_in, 16)
            sp.dma_start(c_n[:, :, :, :], C.rearrange("(a h) n r -> h a n r", a=2)).then_inc(par_in, 16)

            def load_x(p, h):
                sp.dma_start(x_in[p][:, :, :], x[:, bass.ds(h, 2), :]).then_inc(x_arrived[p], 16)

            for p in range(XS):
                load_x(p, 2 * p)

            def refill(t):
                for p in range(XS):
                    h = (t * XS + p) * 2
                    sp.wait_ge(ut_ready, h - 2 * XS + 2)
                    load_x(p, h)

            refill(1)
            sp.dma_start(cen_nat, centroids).then_inc(cen_in, 16)
            sp.dma_start(len_i[:, :], lengths.rearrange("(a b) -> a b", a=1).to_broadcast((P, P))).then_inc(len_in, 16)
            sp.wait_ge(consts, 4)
            sp.dma_start(scratch[:, L:KR], zero[:, :]).then_inc(tail_out, 16)
            refill(2)
            sp.wait_ge(tail_out, 16)
            sp.wait_ge(k_out, 32)
            for s in range(G):
                sp.dma_start(toep[s][:, :], toep_source(s)).then_inc(toep_arrived[s], 16)
            refill(3)
            sp.dma_start(w_nat, weight.rearrange("(j p) l -> p j l", p=P)).then_inc(w_in, 16)
            sp.dma_start(bias_b[:, :], bias.rearrange("(a o) -> a o", a=1).to_broadcast((P, O))).then_inc(row_in, 16)
            sp.dma_start(asg_i[:, :], assignments.rearrange("(a o) -> a o", a=1).to_broadcast((NC, O))).then_inc(row_in, 16)
            with sp.Fori(1, T) as t:
                for s in range(G):
                    h = t * G + s
                    sp.wait_ge(t_ready, h - G + 1)
                    sp.dma_start(toep[s][:, :], toep_source(h)).then_inc(toep_arrived[s], 16)
            sp.wait_ge(ut_ready, H)

            def reload_x(p, h):
                sp.dma_start(x_in[p][:, :, :], x[:, bass.ds(h, 2), :]).then_inc(x_back[p], 16)

            for p in range(2):
                reload_x(p, 2 * p)
            with sp.Fori(1, T) as t:
                for p in range(2):
                    h = t * G + 2 * p
                    sp.wait_ge(result_ready, h - G + 2)
                    sp.dma_start(out[:, bass.ds(h - G, 2), :], result[p]).then_inc(stored[p], 16)
                    reload_x(p, h)
            for s in range(G):
                sp.wait_ge(result_ready, H - G + s + 1)
                sp.dma_start(out[:, H - G + s, :], result[s // 2][:, s % 2, :]).then_inc(stored[s // 2], 16)
            for p in range(2):
                sp.wait_ge(stored[p], 16 * (T + 1))

        @block.gpsimd
        def _(pool):
            made = [0]

            def link(ins):
                made[0] += 1
                ins.then_inc(pool_step, 1)
                pool.wait_ge(pool_step, made[0])

            link(pool.memset(ident[:, :], 0.0))
            pool.affine_select(out=ident[:, :], in_=ident[:, :], compare_op=ALU.not_equal, fill=1.0, base=0,
                               pattern=[[-1, P]], channel_multiplier=1).then_inc(consts, 1)
            pool.iota(lval[:, 0:LC], [[-1, LC]], base=LC - 1, channel_multiplier=0,
                      allow_small_or_imprecise_dtypes=True).then_inc(consts, 1)
            pool.iota(lval[:, LC:LV], [[-LC, LA]], base=L - LC, channel_multiplier=0,
                      allow_small_or_imprecise_dtypes=True).then_inc(consts, 1)
            pool.memset(zero[:, :], 0.0).then_inc(consts, 1)
            pool.memset(half_pi[:, :], math.pi / 2).then_inc(consts, 1)
            pool.iota(pos[:, :], [[P, J]], base=P - 1, channel_multiplier=-1,
                      allow_small_or_imprecise_dtypes=True).then_inc(consts, 1)
            pool.iota(clus[:, :], [[0, 1]], base=0, channel_multiplier=1,
                      allow_small_or_imprecise_dtypes=True).then_inc(consts, 1)
            pool.memset(best[:, :, :], 0.0).then_inc(best_ready, 1)
            link(pool.memset(d_at0[:, :], 0.0))
            for i in (LA - 1, 2 * LA - 1):
                pool.dma_start(d_at0[i:i + 1, :], D.rearrange("(a h) -> a h", a=1)).then_inc(d_in, 16)
            pool.wait_ge(dta_ready, 1)
            pool.tensor_tensor(grow, dta_r[:, :].unsqueeze(2).to_broadcast((P, HH, LV)),
                               lval[:, :].unsqueeze(1).to_broadcast((P, HH, LV)), ALU.mult).then_inc(grow_ready, 1)
            pool.wait_ge(osc_ready, 2)
            pool.wait_ge(mag_ready, 1)
            for i in range(2):
                pool.tensor_tensor(f_c[:, i, :, :], osc[:, i, :, 0:LC], mag[:, :, 0:LC], ALU.mult).then_inc(f_ready, 1)
            pool.wait_ge(cen_in, 16)
            for j in range(J):
                pool.tensor_copy(cen_rev[:, j * P:(j + 1) * P], cen_nat[:, back(j)]).then_inc(rev_ready, 1)

            def low_t(h, s):
                pool.wait_ge(t_hi_ready, h + 1)
                pool.tensor_tensor(t_lo[s][:, :], toep[s][:, :], t_hi[s][:, :].bitcast(F32), ALU.subtract).then_inc(t_ready, 1)

            def probabilities(t):
                hs = slice(t * G, t * G + G) if isinstance(t, int) else bass.ds(t * G, G)
                pool.wait_ge(inv_ready, t + 1)
                pool.tensor_tensor(prob[:, :, :], e[:, :, :], inv[:, hs].unsqueeze(2).to_broadcast((P, G, NC)),
                                   ALU.mult).then_inc(prob_ready, 1)

            def low_y(h, s):
                pool.wait_ge(y_hi_ready, h + 1)
                pool.tensor_tensor(y_lo[s][:, :], xy[:, h, :], y_hi[s][:, :].bitcast(F32), ALU.subtract).then_inc(y_split, 1)

            for s in range(3):
                low_t(s, s)
            for s in range(G):
                low_t(s + 3, (s + 3) % G)
            with pool.Fori(1, T - 1) as t:
                for s in range(G):
                    if s == 2:
                        probabilities(t - 1)
                    low_t(t * G + s + 3, (s + 3) % G)
            low_t(H - 1, G - 1)
            for s in range(G):
                if s == 2:
                    probabilities(T - 2)
                low_y(s, s)
            probabilities(T - 1)
            with pool.Fori(1, T) as t:
                for s in range(G):
                    low_y(t * G + s, s)

        @block.scalar
        def _(act):
            act.dma_start(aim_n[:, :, :], A_imag.rearrange("(a h) n -> h a n", a=2)).then_inc(par_in, 16)
            for i in range(2):
                act.dma_start(ex[i * N:(i + 1) * N, 1, :],
                              log_dt[i * HH:(i + 1) * HH].rearrange("(a h) -> a h", a=1).to_broadcast((N, HH))).then_inc(dt_in, 16)
            act.preload_act_table_set("silu_and_others")
            act.wait_ge(dta_ready, 1)
            act.activation(th[:, :], dta_r[:, :], ACT.Tanh, scale=0.5).then_inc(small_ready, 1)
            act.wait_ge(turn_ready, 1)
            act.activation(s1[:, :], frac[:, :], ACT.Sin, scale=TWO_PI).then_inc(small_ready, 1)
            act.activation(sh[:, :], frac[:, :], ACT.Sin, scale=TWO_PI / 2).then_inc(small_ready, 1)

            def keep_u(t, s):
                h = t * G + s
                act.wait_ge(ut_ready, h + 1)
                act.activation(xy[:, h, :], xt[s][:, :], ACT.Copy).then_inc(ut_kept[s], 1)

            for s in range(G):
                keep_u(0, s)
            act.wait_ge(phase_ready, 1)
            act.activation(osc[:, 1, :, :], phase, ACT.Sin, scale=TWO_PI).then_inc(osc_ready, 1)
            act.wait_ge(phase_ready, 2)
            act.wait_ge(consts, 5)
            act.activation(osc[:, 0, :, :], absph, ACT.Sin, scale=-TWO_PI, bias=half_pi[:, :]).then_inc(osc_ready, 1)
            act.wait_ge(grow_ready, 1)
            act.activation(mag, grow, ACT.Exp).then_inc(mag_ready, 1)
            for s in range(G):
                keep_u(1, s)
            for s in range(0, G, 2):
                keep_u(2, s)
            act.wait_ge(d_added, 1)
            act.activation(k_sb[:, 0, :], spare[0][0:2 * LA, :], ACT.Copy).then_inc(k_copied, 1)
            act.wait_ge(k_copied, 2)
            for i in range(2):
                act.dma_start(scratch[i:H:2, 0:L].rearrange("g (a c) -> a g c", a=LA),
                              k_sb[i * LA:(i + 1) * LA, :, :].rearrange("p b (g i c) -> p (b g) i c", i=2, c=LC)[:, :, i, :])\
                   .then_inc(k_out, 16)
            with act.Fori(3, EARLY // G) as t:
                for s in range(0, G, 2):
                    keep_u(t, s)

            def high_t(t, s, first=False):
                h = t * G + s
                act.wait_ge(toep_arrived[s], 16 * (t + 1))
                if not first:
                    act.wait_ge(conv_done, h - G + 1)
                act.activation(t_hi[s][:, :], toep[s][:, :], ACT.Copy).then_inc(t_hi_ready, 1)

            def high_u(h, s, first=False):
                if not first:
                    act.wait_ge(conv_done, h - 1)
                act.activation(u_hi[s % 2][:, :], xy[:, h, :], ACT.Copy).then_inc(u_hi_ready, 1)

            def keep_y(h, s, waited=False):
                if not waited:
                    act.wait_ge(y_ready, h + 1)
                act.activation(xy[:, h, :], y_m[s % 2][:, :], ACT.Copy).then_inc(y_kept, 1)

            def exps(t):
                act.wait_ge(above_ready, t + 1)
                if not isinstance(t, int):
                    act.wait_ge(prob_ready, t)
                elif t > 0:
                    act.wait_ge(prob_ready, t)
                act.activation(e[:, :, :], above[:, :, :], ACT.Exp, scale=1.0 / TEMPERATURE).then_inc(e_ready, 1)

            def high_y(h, s, first=False):
                if not first:
                    act.wait_ge(dense_done, h - G + 1)
                act.activation(y_hi[s][:, :], xy[:, h, :], ACT.Copy).then_inc(y_hi_ready, 1)

            for s in range(2):
                act.wait_ge(ut_kept[s], 1)
            high_u(0, 0, True)
            high_u(1, 1, True)
            act.wait_ge(wt_ready, 1)
            act.activation(cenT[:, :, :], yt[1][:, 0:J * NC].rearrange("p (j c) -> p j c", c=NC), ACT.Copy).then_inc(cen_copied, 1)
            for s in range(3):
                high_t(0, s, True)

            def channels(t):
                for s in range(G):
                    high_u(t * G + s + 2, s)
                    if s == 1 and not (isinstance(t, int) and t == 0):
                        exps(t - 1)
                    if isinstance(t, int) and t == 0:
                        act.wait_ge(ut_ready, EARLY + 2 * s + 1)
                        act.activation(xy[:, EARLY + 2 * s, :], ut[0][:, :], ACT.Copy).then_inc(ut_kept[0], 1)
                    act.wait_ge(y_ready, t * G + s + 1)
                    high_t(t + (s + 3) // G, (s + 3) % G, isinstance(t, int) and t == 0 and s == 0)
                    keep_y(t * G + s, s, True)
                    if isinstance(t, int) and t == 0 and s >= 2:
                        act.wait_ge(w_in, 16)
                        for j in (2 * s - 4, 2 * s - 3):
                            act.activation(w_rev[:, :, j * P:(j + 1) * P], w_nat[:, :, back(j)], ACT.Copy).then_inc(w_rev_ready, 1)
                    if isinstance(t, int) and t == 1:
                        act.wait_ge(wt_ready, s + 2)
                        act.activation(w_hi[:, s, :], bank[s][:, :], ACT.Copy).then_inc(w_hi_ready, 1)

            channels(0)
            channels(1)
            with act.Fori(2, T - 1) as t:
                channels(t)
            for s in range(G):
                if s < G - 2:
                    high_u(H - G + s + 2, s)
                if s == 1:
                    exps(T - 2)
                keep_y(H - G + s, s)
                if s == 0:
                    high_t(T - 1, G - 1)
                high_y(s, s, True)
            exps(T - 1)
            act.wait_ge(y_kept, H)
            with act.Fori(1, T) as t:
                for s in range(G):
                    high_y(t * G + s, s)

        @block.vector
        def _(dve):
            made = [0]

            def link(ins):
                made[0] += 1
                ins.then_inc(dve_step, 1)
                dve.wait_ge(dve_step, made[0])

            tt, ts, stt = nc.vector.tensor_tensor, nc.vector.tensor_scalar, nc.vector.scalar_tensor_tensor
            dve.wait_ge(params_t, 1)
            pt = yt[0][:, 0:4 * HH].rearrange("p (k h) -> p k h", h=HH)
            nc.vector.tensor_copy(ex[:, 0, :], pt[:, 0, :])
            link(nc.vector.tensor_copy(par[:, :, :], pt[:, 1:4, :]))
            dve.wait_ge(dt_in, 32)
            v = ex[:, :, :]
            kf, k, r, q, k2 = (tmp[i][:, :, :] for i in range(5))
            c = exp_coefficients()
            aim, c_re, c_im = par[:, 0, :], par[:, 1, :], par[:, 2, :]
            link(ts(v, v, -87.0, 88.0, ALU.max, ALU.min))
            link(ts(kf, v, 1.0 / math.log(2.0), MAGIC, ALU.mult, ALU.add))
            link(ts(k, kf, MAGIC, None, ALU.subtract))
            link(stt(r, k, -LN2_HI, v, ALU.mult, ALU.add))
            link(stt(r, k, -LN2_LO, r, ALU.mult, ALU.add))
            ts(k2.bitcast(I32), kf.bitcast(I32), MAGIC_BITS_SHIFT, None, ALU.logical_shift_left)
            link(ts(q, r, c[-1], None, ALU.mult))
            for cj in c[-2::-1]:
                link(stt(q, q, cj, r, ALU.add, ALU.mult))
            link(ts(q, q, 1.0, None, ALU.add))
            link(tt(v.bitcast(I32), q.bitcast(I32), k2.bitcast(I32), ALU.add))
            e_re, dt = ex[:, 0, :], ex[:, 1, :]
            b, w2 = tmp[0][:, 0, :], tmp[0][:, 1, :]
            tt(b, aim, dt, ALU.mult)
            stt(dta_r[:, :], e_re, -1.0, dt, ALU.mult, ALU.mult).then_inc(dta_ready, 1)
            link(tt(abs2[:, 0, :], e_re, e_re, ALU.mult))
            ts(turns[:, :], b, 1.0 / (2 * math.pi), None, ALU.mult)
            link(tt(abs2[:, 1, :], aim, aim, ALU.mult))
            ts(w2, turns[:, :], MAGIC, MAGIC, ALU.add, ALU.subtract)
            link(tt(abs2[:, 0, :], abs2[:, 0, :], abs2[:, 1, :], ALU.add))
            tt(frac[:, :], turns[:, :], w2, ALU.subtract).then_inc(turn_ready, 1)
            dve.wait_ge(consts, 3)
            link(tt(phase, turns[:, :].unsqueeze(2).to_broadcast((P, HH, LV)),
                    lval[:, :].unsqueeze(1).to_broadcast((P, HH, LV)), ALU.mult))
            link(ts(whole, phase, MAGIC, MAGIC, ALU.add, ALU.subtract))
            tt(phase, phase, whole, ALU.subtract).then_inc(phase_ready, 1)
            T1, T2, T3, T4, T5, T6, T7, T8 = (tmp[1 + i // 2][:, i % 2, :] for i in range(8))
            nc.vector.reciprocal(T1, abs2[:, 0, :])
            dve.wait_ge(phase_ready, 1)
            ts(absph.bitcast(I32), phase.bitcast(I32), 0x7FFFFFFF, None, ALU.bitwise_and).then_inc(phase_ready, 1)
            dve.wait_ge(small_ready, 3)
            link(ts(T3, th[:, :], -1.0, 1.0, ALU.mult, ALU.add))
            stt(T2, sh[:, :], -2.0, sh[:, :], ALU.mult, ALU.mult)
            link(nc.vector.reciprocal(T3, T3))
            link(stt(T3, th[:, :], 2.0, T3, ALU.mult, ALU.mult))
            stt(T5, T3, 1.0, s1[:, :], ALU.add, ALU.mult)
            link(stt(T4, T2, 1.0, T3, ALU.add, ALU.mult))
            link(tt(T4, T4, T2, ALU.add))
            tt(T6, T5, aim, ALU.mult)
            tt(T8, T5, e_re, ALU.mult)
            tt(T7, T4, e_re, ALU.mult)
            link(tt(T3, T4, aim, ALU.mult))
            tt(T6, T6, T7, ALU.subtract)
            link(tt(T3, T3, T8, ALU.add))
            stt(T6, T6, 2.0, T1, ALU.mult, ALU.mult)
            link(stt(T7, T3, -2.0, T1, ALU.mult, ALU.mult))
            tt(T1, c_re, T6, ALU.mult)
            tt(T2, c_im, T7, ALU.mult)
            tt(T3, c_re, T7, ALU.mult)
            link(tt(T4, c_im, T6, ALU.mult))
            tt(coef[:, 0, :], T1, T2, ALU.subtract)
            link(tt(coef[:, 1, :], T3, T4, ALU.add))
            dve.wait_ge(osc_ready, 2)
            dve.wait_ge(mag_ready, 1)
            for i in range(2):
                last = tt(e_a[:, i, :, :], osc[:, i, :, LC:LV], mag[:, :, LC:LV], ALU.mult)
            link(last)
            for i in range(2):
                tt(e_p[:, i, :, :], e_a[:, i, :, :], coef[:, 0, :].unsqueeze(2).to_broadcast((P, HH, LA)), ALU.mult)
                last = tt(e_q[:, i, :, :], e_a[:, i, :, :], coef[:, 1, :].unsqueeze(2).to_broadcast((P, HH, LA)), ALU.mult)
            link(last)
            tt(g_a[:, 0, :, :], e_p[:, 0, :, :], e_q[:, 1, :, :], ALU.subtract)
            stt(g_a[:, 1, :, :].rearrange("p h a -> p (h a)"), e_p[:, 1, :, :].rearrange("p h a -> p (h a)"), -1.0,
                e_q[:, 0, :, :].rearrange("p h a -> p (h a)"), ALU.mult, ALU.subtract).then_inc(g_ready, 1)
            for s in range(1, G, 2):
                dve.wait_ge(ut_ready, 2 * G + s + 1)
                nc.vector.tensor_copy(xy[:, 2 * G + s, :], xt[s][:, :]).then_inc(ut_kept[s], 1)
            dve.wait_ge(len_in, 16)
            dve.wait_ge(consts, 7)
            link(nc.vector.tensor_copy(len_f[:, :], len_i[:, :]))
            for j in range(J):
                ts(mask[:, j, :], len_f[:, :], pos[:, j:j + 1], None, ALU.is_gt).then_inc(mask_ready, 1)
            mask_f = mask[:, :, :].rearrange("p j b -> p (j b)")
            dve.wait_ge(k_ready, 1)
            dve.wait_ge(d_in, 32)
            for i in range(2):
                at0 = spare[i][0:2 * LA, :].rearrange("a (h c) -> a h c", c=LC)[:, :, LC - 1]
                last = tt(at0, at0, d_at0[:, HH * i:HH * (i + 1)], ALU.add)
            last.then_inc(d_added, 1)
            dve.wait_ge(d_added, 1)
            nc.vector.tensor_copy(k_sb[:, 1, :], spare[1][0:2 * LA, :]).then_inc(k_copied, 1)

            def keep_u(t, s):
                h = t * G + s
                dve.wait_ge(ut_ready, h + 1)
                nc.vector.tensor_copy(xy[:, h, :], xt[s][:, :]).then_inc(ut_kept[s], 1)

            with dve.Fori(3, EARLY // G) as t:
                for s in range(1, G, 2):
                    keep_u(t, s)

            def low_u(h, s):
                dve.wait_ge(u_hi_ready, h + 1)
                tt(u_lo[s % 2][:, :], xy[:, h, :], u_hi[s % 2][:, :].bitcast(F32), ALU.subtract).then_inc(u_ready, 1)

            low_u(0, 0)
            low_u(1, 1)
            dve.wait_ge(mask_ready, J)

            def mask_y(h, s, first=False):
                dve.wait_ge(conv_done, h + 1)
                if not first:
                    dve.wait_ge(logits_done, h - 1)
                    dve.wait_ge(y_kept, h - 1)
                tt(y_m[s % 2][:, :], yt[s % 2][:, :], mask_f, ALU.mult).then_inc(y_ready, 1)

            logits_ps = lg[0][:, 0:G * NC].rearrange("p (g c) -> p g c", c=NC)
            base = made[0]

            def softmax_above(t, hs):
                dve.wait_ge(logits_done, (t + 1) * G)
                nc.vector.reduce_max(top[:, hs], logits_ps, AX.X).then_inc(dve_step, 1)
                dve.wait_ge(dve_step, base + 2 * t + 1)
                tt(above[:, :, :], logits_ps, top[:, hs].unsqueeze(2).to_broadcast((P, G, NC)),
                   ALU.subtract).then_inc(above_ready, 1)

            def softmax_sum(t, hs):
                dve.wait_ge(e_ready, t + 1)
                nc.vector.reduce_sum(total[:, hs], e[:, :, :], AX.X).then_inc(dve_step, 1)
                dve.wait_ge(dve_step, base + 2 * t + 2)
                nc.vector.reciprocal(inv[:, hs], total[:, hs]).then_inc(inv_ready, 1)

            def softmax_best(t):
                dve.wait_ge(prob_ready, t + 1)
                dve.wait_ge(best_ready, t + 1)
                tt(best[:, :, :], best[:, :, :], prob[:, :, :], ALU.max).then_inc(best_ready, 1)

            for s in range(G):
                mask_y(s, s, s < 2)
                low_u(s + 2, s)
                dve.wait_ge(ut_ready, EARLY + 2 * s + 2)
                nc.vector.tensor_copy(xy[:, EARLY + 2 * s + 1, :], ut[1][:, :]).then_inc(ut_kept[1], 1)

            def channels(t, hs):
                for s in range(G):
                    mask_y(t * G + s, s)
                    low_u(t * G + s + 2, s)
                    if s == 0:
                        softmax_above(t - 1, hs)
                    if s == 1:
                        softmax_sum(t - 1, hs)
                    if s == 2:
                        softmax_best(t - 1)
                    if isinstance(t, int):
                        dve.wait_ge(w_hi_ready, s + 1)
                        tt(w_lo[:, s, :], bank[s][:, :], w_hi[:, s, :].bitcast(F32), ALU.subtract).then_inc(w_lo_ready, 1)

            channels(1, slice(0, G))
            dve.wait_ge(row_in, 32)
            dve.wait_ge(consts, 7)
            nc.vector.tensor_copy(asg_f[:, :], asg_i[:, :]).then_inc(asg_ready, 1)
            dve.wait_ge(asg_ready, 1)
            ts(onehot[:, :], asg_f[:, :], clus[:, :], None, ALU.is_equal)
            with dve.Fori(2, T - 1) as t:
                channels(t, bass.ds(t * G - G, G))
            hs = slice(H - 2 * G, H - G)
            for s in range(G):
                mask_y(H - G + s, s)
                if s < G - 2:
                    low_u(H - G + s + 2, s)
                if s == 0:
                    softmax_above(T - 2, hs)
                if s == 1:
                    softmax_sum(T - 2, hs)
                if s == 2:
                    softmax_best(T - 2)
            hs = slice(H - G, H)
            softmax_above(T - 1, hs)
            softmax_sum(T - 1, hs)
            softmax_best(T - 1)
            made[0] = base + 2 * T
            dve.wait_ge(inv_ready, T)
            ts(query[:, :], inv[:, :], THRESHOLD, None, ALU.is_gt)
            dve.wait_ge(best_ready, T + 1)
            nc.vector.reduce_max(best1[:, :], best[:, :, :].rearrange("p g c -> p c g"), AX.X).then_inc(sel_ready, 1)

            def add_bias(h, s, first=False):
                dve.wait_ge(dense_done, h + 1)
                if not first:
                    dve.wait_ge(chosen_ready, h - G + 1)
                tt(dense[s], bank[s][:, :], bias_b[:, :], ALU.add).then_inc(dense_read, 1)

            def choose(h, s, first=False):
                dve.wait_ge(dense_read, h + 1)
                if not first:
                    dve.wait_ge(result_ready, h - 1)
                stt(chosen[s % 2], dense[s], query[:, bass.ds(h, 1)], rows[:, :], ALU.mult, ALU.mult).then_inc(chosen_ready, 1)

            def residual(t, s, first=False):
                h = t * G + s
                dve.wait_ge(chosen_ready, h + 1)
                dve.wait_ge(x_back[s // 2], 16 * (t + 1))
                if not first:
                    dve.wait_ge(stored[s // 2], 16 * t)
                tt(result[s // 2][:, s % 2, :], chosen[s % 2], x_in[s // 2][:, s % 2, :], ALU.add).then_inc(result_ready, 1)

            add_bias(0, 0, True)
            dve.wait_ge(best_t, 1)
            link(nc.vector.reduce_max(best_c[:, :], yt[0][0:NC, 0:P], AX.X))
            ts(sel_b[:, :], best_c[:, :].to_broadcast((NC, P)), THRESHOLD, None, ALU.is_gt).then_inc(sel_ready, 1)
            add_bias(1, 1, True)
            add_bias(2, 2, True)
            dve.wait_ge(rows_ps, 1)
            link(nc.vector.tensor_copy(rows[:, :], yt[1][:, :]))
            choose(0, 0, True)
            choose(1, 1, True)
            residual(0, 0, True)
            add_bias(3, 3, True)
            choose(2, 2)
            residual(0, 1, True)
            choose(3, 3)
            residual(0, 2, True)
            add_bias(4, 0)

            def channel(t, s, last=False):
                choose(t * G + s, s)
                residual(t + (s - 1) // G, (s - 1) % G, isinstance(t, int) and t == 1 and s == 0)
                if not last:
                    add_bias(t * G + s + 1, (s + 1) % G)

            for s in range(G):
                channel(1, s)
            with dve.Fori(2, T - 1) as t:
                for s in range(G):
                    channel(t, s)
            for s in range(G):
                channel(T - 1, s, s == G - 1)
            residual(T - 1, G - 1)

        @block.tensor
        def _(pe):
            mm, tr = nc.tensor.matmul, nc.tensor.transpose
            pe.wait_ge(consts, 1)
            pe.wait_ge(par_in, 48)
            flat = "h a n -> h (a n)"
            for i, src in enumerate((lar_n[:, :, :].rearrange(flat), aim_n[:, :, :].rearrange(flat),
                                     c_n[:, :, :, 0].rearrange(flat), c_n[:, :, :, 1].rearrange(flat))):
                last = tr(yt[0][:, i * HH:(i + 1) * HH], src, ident[0:HH, 0:HH])
            last.then_inc(params_t, 1)

            def transposes(t, m):
                if isinstance(t, int) and t == 0 and m < G:
                    pe.wait_ge(x_arrived[m // 2], 16)
                else:
                    pe.wait_ge(x_arrived[m // 2], 16 * (t + 1))
                    pe.wait_ge(ut_kept[m % G], 2 * t + m // G)
                for j in range(J):
                    last = tr(xt[m % G][:, j * P:(j + 1) * P], x_in[m // 2][:, m % 2, j * P:(j + 1) * P], ident[:, :])
                last.then_inc(ut_ready, 1)

            for m in range(2 * XS):
                transposes(0, m)
            for m in range(G):
                transposes(1, m)
            pe.wait_ge(f_ready, 2)
            pe.wait_ge(g_ready, 1)
            for a in range(2):
                rows_a = slice(a * N, (a + 1) * N)
                for g in range(HH // 2):
                    pair = slice(2 * g, 2 * g + 2)
                    for i in range(2):
                        last = mm(spare[a][0:2 * LA, g * 2 * LC:(g + 1) * 2 * LC],
                                  g_a[rows_a, i, pair, :].rearrange("p h a -> p (h a)"),
                                  f_c[rows_a, i, pair, :].rearrange("p h c -> p (h c)"), start=(i == 0), stop=(i == 1))
            last.then_inc(k_ready, 1)
            for m in range(G, 2 * XS):
                transposes(1, m)
            with pe.Fori(2, EARLY // (2 * XS)) as t:
                for m in range(2 * XS):
                    transposes(t, m)
            pe.wait_ge(rev_ready, J)
            for j in range(J):
                last = tr(yt[1][:, j * NC:(j + 1) * NC], cen_rev[:, j * P:(j + 1) * P], ident[0:NC, 0:NC])
            last.then_inc(wt_ready, 1)

            def convolution(t, s, first=False):
                h = t * G + s
                pe.wait_ge(u_ready, h + 1)
                pe.wait_ge(t_ready, h + 1)
                if not first:
                    pe.wait_ge(y_ready, h - 1)
                for d in range(J):
                    blocks = slice((J - 1 - d) * P, (J - d) * P)
                    for i, (tp, u) in enumerate(((t_hi, u_hi), (t_hi, u_lo), (t_lo, u_hi))):
                        last = mm(yt[s % 2][:, d * P:], tp[s][:, blocks], u[s % 2][:, 0:(J - d) * P],
                                  start=(d == 0 and i == 0), stop=(d == J - 1 and i == 2))
                last.then_inc(conv_done, 1)

            def logits(h, s):
                pe.wait_ge(y_ready, h + 1)
                for j in range(J):
                    last = mm(lg[0][:, s * NC:(s + 1) * NC], y_m[s % 2][:, j * P:(j + 1) * P], cenT[:, j, :],
                              start=(j == 0), stop=(j == J - 1))
                last.then_inc(logits_done, 1)

            for s in range(G):
                convolution(0, s, s < 2)
                if s == 0:
                    pe.wait_ge(cen_copied, 1)
                    pe.wait_ge(ut_kept[2], EARLY // G)
                else:
                    logits(s - 1, s - 1)
                pe.wait_ge(x_arrived[s], 16 * (EARLY // (2 * XS) + 1))
                for i in range(2):
                    pe.wait_ge(ut_kept[i], EARLY // G + s)
                    for j in range(J):
                        last = tr(ut[i][:, j * P:(j + 1) * P], x_in[s][:, i, j * P:(j + 1) * P], ident[:, :])
                    last.then_inc(ut_ready, 1)

            def channels(t):
                for s in range(G):
                    convolution(t, s)
                    if s == 1:
                        pe.wait_ge(above_ready, t)
                    logits(t * G + s - 1, (s - 1) % G)
                    if isinstance(t, int):
                        pe.wait_ge(w_rev_ready, J)
                        for o in range(O // P):
                            last = tr(bank[s][:, o * P:(o + 1) * P], w_rev[:, o, s * P:(s + 1) * P], ident[:, :])
                        last.then_inc(wt_ready, 1)

            pe.wait_ge(k_copied, 2)
            for i in range(2):
                pe.wait_ge(ut_kept[i], EARLY // G + G)
            channels(1)
            with pe.Fori(2, T) as t:
                channels(t)
            logits(H - 1, G - 1)

            def layer(h, s, first=False):
                pe.wait_ge(y_split, h + 1)
                if not first:
                    pe.wait_ge(dense_read, h - G + 1)
                for j in range(J):
                    js = slice(j * P, (j + 1) * P)
                    mm(bank[s][:, :], y_hi[s][:, js], w_hi[:, j, :], start=(j == 0), stop=False)
                    mm(bank[s][:, :], y_hi[s][:, js], w_lo[:, j, :], start=False, stop=False)
                    last = mm(bank[s][:, :], y_lo[s][:, js], w_hi[:, j, :], start=False, stop=(j == J - 1))
                last.then_inc(dense_done, 1)

            pe.wait_ge(w_lo_ready, J)
            layer(0, 0, True)
            layer(1, 1, True)
            pe.wait_ge(sel_ready, 1)
            tr(yt[0][0:NC, 0:P], best1[:, :], ident[:, :]).then_inc(best_t, 1)
            layer(2, 2, True)
            pe.wait_ge(sel_ready, 2)
            mm(yt[1][:, :], sel_b[:, :], onehot[:, :], start=True, stop=True).then_inc(rows_ps, 1)
            layer(3, 3, True)
            with pe.Fori(1, T) as t:
                for s in range(G):
                    layer(t * G + s, s)


_INS = ["x", "itok_B_8_3872", "L0_cond_log_dt", "L0_cond_C", "L0_cond_log_A_real", "L0_cond_A_imag", "L0_cond_D",
        "L0_ffn_weight", "L0_ffn_bias", "L0_ffn_centroids", "L0_ffn_assignments"]


def kernel(**inputs):
    import numpy as _np
    import concourse.bacc as _bacc
    from concourse import mybir as _mybir
    from concourse.bass_utils import run_bass_kernel_spmd as _run

    nc = _bacc.Bacc("TRN2", target_bir_lowering=False, num_devices=1)
    arrays, args = {}, []
    for name in _INS:
        a = _np.ascontiguousarray(inputs[name])
        arrays[f"in_{name}"] = a
        args.append(nc.dram_tensor(f"in_{name}", a.shape, _mybir.dt.from_np(a.dtype), kind="ExternalInput").ap())
    out = nc.dram_tensor("out_0", (P, H, L), _mybir.dt.float32, kind="ExternalOutput").ap()
    program(nc, *args, out)
    r = _run(nc, [arrays], core_ids=[0])
    return r.results[0]["out_0"]
```

```python
import math
from contextlib import ExitStack

import numpy as np
import concourse.bass as bass
from concourse import mybir

F32 = mybir.dt.float32
F32R = mybir.dt.float32r
BF16 = mybir.dt.bfloat16
I32 = mybir.dt.int32
ALU = mybir.AluOpType
ACT = mybir.ActivationFunctionType
AX = mybir.AxisListType

P = 128
H = 32
L = 512
J = L // P
N = 64
O = 512
NC = 64
LC = 32
LA = L // LC
LV = LC + LA
XS = 12
XB = 4
EARLY = 26
HELD = 12
BEFORE_K = 11
HH = H // 2
TAIL = P
KR = L + TAIL
G = 4
T = H // G
UT = 4
U = UT * G
OH = O // 2
CH = NC // 2
MAGIC = 1.5 * 2.0 ** 23
MANTISSA = 23
TWO_PI = float(np.nextafter(np.float32(2 * math.pi), np.float32(0)))
LN2_HI = 0.693359375
LN2_LO = math.log(2.0) - LN2_HI
TEMPERATURE = 0.1
THRESHOLD = 0.01


def exp_coefficients(degree=6):
    n = degree
    nodes = np.cos((2 * np.arange(n) + 1) * np.pi / (2 * n)) * (math.log(2.0) / 2 * 1.02)
    a = np.vander(nodes, n, increasing=True)
    return [float(v) for v in np.linalg.solve(a, np.expm1(nodes) / nodes)]


def program(nc, x, lengths, log_dt, C, log_A_real, A_imag, D, weight, bias, centroids, assignments, out):
    ctx = ExitStack()
    with ctx:
        def sb(name, shape, dt=F32):
            return ctx.enter_context(nc.sbuf_tensor(name, shape, dt))

        def ps(name, shape, dt=F32):
            return ctx.enter_context(nc.psum_tensor(name, shape, dt))

        def sem(name):
            return ctx.enter_context(nc.semaphore(name))

        scratch = nc.dram_tensor("kernel_reversed", (H, KR), F32, kind="Internal").ap()

        WORK = 8192
        work = sb("work", [P, WORK])

        def carve(start, parts, shape):
            n = int(np.prod(shape))
            assert start + n <= WORK
            piece = work[0:parts, start:start + n]
            if len(shape) == 2:
                piece = piece.rearrange("p (a b) -> p a b", b=shape[1])
            if len(shape) == 3:
                piece = piece.rearrange("p (a b c) -> p a b c", b=shape[1], c=shape[2])
            return piece, start + n

        phase, at = carve(0, P, (HH, LV))
        whole, at = carve(at, P, (HH, LV))
        absph, at = carve(at, P, (HH, LV))
        grow, at = carve(at, P, (HH, LV))
        mag, at = carve(at, P, (HH, LV))
        osc, at = carve(at, P, (2, HH, LV))
        f_c, at = carve(at, P, (2, HH, LC))
        e_a, _ = carve(0, P, (2, HH, LA))
        e_p, _ = carve(HH * LV, P, (2, HH, LA))
        e_q, _ = carve(2 * HH * LV, P, (2, HH, LA))
        g_a, at = carve(at, P, (2, HH, 2 * LA))
        k_sb, at = carve(at, 2 * LA, (HH * LC,))
        w_nat, at = carve(0, P, (J, L))
        w_rev, at = carve(at, P, (J, L))
        xw, at = carve(0, P, (H - U, L))

        ident = sb("ident", [P, P])
        lval = sb("lval", [P, LV])
        pos = sb("pos", [P, J])
        clus = sb("clus", [NC, 1])
        zero = sb("zero", [H, TAIL])
        half_pi = sb("half_pi", [P, 1])

        lar_n = sb("lar_n", [HH, 2, N])
        aim_n = sb("aim_n", [HH, 2, N])
        c_n = sb("c_n", [HH, 2, N, 2])
        d_at0 = sb("d_at0", [2 * LA, HH])
        len_i = sb("len_i", [P, P], I32)
        len_f = sb("len_f", [P, P])
        mask = sb("mask", [P, J, P])
        w_hi = sb("w_hi", [P, J, 2, OH + CH], F32R)
        w_lo = sb("w_lo", [P, J, 2, OH + CH], F32R)
        cenT = sb("cenT", [P, J, NC])
        bias_b = sb("bias_b", [P, O])
        asg_i = sb("asg_i", [NC, O], I32)
        asg_f = sb("asg_f", [NC, O])
        onehot = sb("onehot", [NC, O], BF16)

        ex = sb("ex", [P, 2, HH])
        par = sb("par", [P, 3, HH])
        tmp = [sb(f"tmp{i}", [P, 2, HH]) for i in range(5)]
        small = sb("small", [P, 12, HH])
        abs2 = sb("abs2", [P, 2, HH])
        dta_r = sb("dta_r", [P, HH])
        turns = sb("turns", [P, HH])
        frac = sb("frac", [P, HH])
        s1 = sb("s1", [P, HH])
        sh = sb("sh", [P, HH])
        th = sb("th", [P, HH])
        coef = sb("coef", [P, 2, HH])

        x_in = [sb(f"x_in{i}", [P, 2, L])[:, :, :] for i in range(XB)]
        xy = sb("xy", [P, H, J * P])
        x_in += [xy[:, H - 2 * (XS - i):H - 2 * (XS - i) + 2, :] for i in range(XB, XS)]
        toeps = sb("toeps", [P, G, L])
        toep = [toeps[:, i, :] for i in range(G)]
        t_hi = [sb(f"t_hi{i}", [P, L], F32R) for i in range(G)]
        t_lo = [sb(f"t_lo{i}", [P, L], F32R) for i in range(G)]
        u_hi = [sb(f"u_hi{i}", [P, J * P], F32R) for i in range(2)]
        u_lo = [sb(f"u_lo{i}", [P, J * P], F32R) for i in range(2)]
        y_hi = [sb(f"y_hi{i}", [P, J * P], F32R)[:, :] for i in range(G)]
        y_lo = [sb(f"y_lo{i}", [P, J * P], F32R)[:, :] for i in range(G)]
        y_m = [sb(f"y_m{i}", [P, J * P]) for i in range(2)]
        cen_nat, cen_rev = (y_m[i][0:NC, :] for i in range(2))

        logits_sb = sb("logits_sb", [P, G, NC])
        top = sb("top", [P, H])
        above = sb("above", [P, G, NC])
        e = sb("e", [P, G, NC])
        total = sb("total", [P, H])
        inv = sb("inv", [P, H])
        prob = sb("prob", [P, G, NC])
        best = sb("best", [P, G, NC])
        best1 = sb("best1", [P, NC])
        query = sb("query", [P, H])
        best_c = sb("best_c", [NC, 1])
        sel_b = sb("sel_b", [NC, P], BF16)
        not_rows = sb("not_rows", [P, O], I32)

        duo = [ps(f"duo{i}", [P, 2, 512]) for i in range(2)]
        bank = [duo[i // 2][:, i % 2, :] for i in range(G)]
        spare, ut = bank[0:2], bank[2:4]
        yt = [ps(f"yt{i}", [P, 512]) for i in range(2)]
        lg = [ps(f"lg{i}", [P, 512]) for i in range(2)]
        xt = [ut[0], ut[1], lg[0], lg[1], yt[0], yt[1]]
        XT = len(xt)

        par_in = sem("par_in")
        dt_in = sem("dt_in")
        d_in = sem("d_in")
        w_in = sem("w_in")
        cen_in = sem("cen_in")
        len_in = sem("len_in")
        row_in = sem("row_in")
        tail_out = sem("tail_out")
        k_out = [sem(f"k_out{i}") for i in range(2)]
        x_arrived = [sem(f"x_arrived{i}") for i in range(XS)]
        x_back = [sem(f"x_back{i}") for i in range(XB)]
        xw_back = sem("xw_back")
        x_last_back = sem("x_last_back")
        toep_arrived = [sem(f"toep_arrived{i}") for i in range(G)]
        stored = sem("stored")
        consts = sem("consts")
        pool_step = sem("pool_step")
        dve_step = sem("dve_step")
        params_t = sem("params_t")
        dta_ready = sem("dta_ready")
        phase_ready = sem("phase_ready")
        turn_ready = sem("turn_ready")
        small_ready = sem("small_ready")
        osc_ready = sem("osc_ready")
        grow_ready = sem("grow_ready")
        mag_ready = sem("mag_ready")
        f_ready = sem("f_ready")
        g_zero = sem("g_zero")
        e_pq_ready = sem("e_pq_ready")
        g_ready = sem("g_ready")
        k_ready = sem("k_ready")
        d_added = sem("d_added")
        k_copied = sem("k_copied")
        rev_ready = sem("rev_ready")
        w_rev_ready = sem("w_rev_ready")
        w_rev_last_ready = sem("w_rev_last_ready")
        wt_ready = sem("wt_ready")
        cen_copied = sem("cen_copied")
        cen_hi_ready = sem("cen_hi_ready")
        w_hi_ready = sem("w_hi_ready")
        w_lo_ready = sem("w_lo_ready")
        ut_ready = sem("ut_ready")
        mask_ready = sem("mask_ready")
        asg_ready = sem("asg_ready")
        ut_kept = [sem(f"ut_kept{i}") for i in range(XT)]
        t_hi_ready = sem("t_hi_ready")
        t_ready = sem("t_ready")
        u_hi_ready = sem("u_hi_ready")
        u_ready = sem("u_ready")
        conv_done = sem("conv_done")
        y_ready = sem("y_ready")
        y_kept = sem("y_kept")
        logits_done = sem("logits_done")
        above_ready = sem("above_ready")
        e_ready = sem("e_ready")
        inv_ready = sem("inv_ready")
        prob_ready = sem("prob_ready")
        query_ready = sem("query_ready")
        best_ready = sem("best_ready")
        best_t = sem("best_t")
        sel_ready = sem("sel_ready")
        rows_ps = sem("rows_ps")
        y_hi_ready = sem("y_hi_ready")
        y_split = sem("y_split")
        dense_done = sem("dense_done")
        dense_read = sem("dense_read")
        duo_done = sem("duo_done")
        taken = sem("taken")
        chosen_ready = sem("chosen_ready")
        mixed = sem("mixed")
        not_rows_ready = sem("not_rows_ready")
        result_ready = sem("result_ready")
        result_w_ready = sem("result_w_ready")
        result_last_ready = sem("result_last_ready")
        last_ready = sem("last_ready")

        def back(j):
            return slice((j + 1) * P - 1, j * P - 1 if j > 0 else None, -1)

        last_half = [bank[G - 1][:, 0:OH], bank[0][:, 0:OH]]
        duos = [b.rearrange("p (i o) -> p i o", i=2) for b in bank]
        cen_halves = cenT[:, :, :].rearrange("p j (i c) -> p j i c", i=2)

        last_bias = y_m[0][:, :]
        rows_sb = y_m[1][:, :]
        x_last = toeps
        rows = yt[1][:, :]

        block = ctx.enter_context(nc.Block())

        def toep_source(h):
            src = scratch[h, 0:L]
            return bass.AP(src.tensor, src.offset, [[1, P], [1, L]])

        HQ = HH // 2
        KH = HQ * LC
        late = H - EARLY
        LATE = [range(min(2 * s, s + late - G), min(2 * s + 2, s + 1 + late - G)) for s in range(G)]
        KEPT_EARLY = [(EARLY - b + XT - 1) // XT for b in range(XT)]
        ACT_KEEPS = ((0, 1), range(2, BEFORE_K), range(BEFORE_K + 1, EARLY, 2))
        DVE_KEEPS = range(BEFORE_K, EARLY, 2)

        def store_kernels(engine, i):
            engine.dma_start(scratch[i * HH:(i + 1) * HH, 0:L].rearrange("g (a c) -> a g c", a=LA),
                             k_sb[i * LA:(i + 1) * LA, :].rearrange("a (g c) -> a g c", c=LC)).then_inc(k_out[i], 16)

        @block.sync
        def _(sp):
            sp.dma_start(lar_n[:, :, :], log_A_real.rearrange("(a h) n -> h a n", a=2)).then_inc(par_in, 16)
            sp.dma_start(c_n[:, :, :, :], C.rearrange("(a h) n r -> h a n r", a=2)).then_inc(par_in, 16)

            def load_x(k):
                if k >= XS:
                    sp.wait_ge(ut_ready, 2 * (k - XS) + 2)
                sp.dma_start(x_in[k % XS], x[:, 2 * k:2 * k + 2, :]).then_inc(x_arrived[k % XS], 16)

            for k in range(4):
                load_x(k)
            sp.wait_ge(consts, 4)
            sp.dma_start(scratch[:, L:KR], zero[:, :]).then_inc(tail_out, 16)
            sp.dma_start(cen_nat, centroids).then_inc(cen_in, 16)
            sp.dma_start(len_i[:, :], lengths.rearrange("(a b) -> a b", a=1).to_broadcast((P, P))).then_inc(len_in, 16)
            for k in range(4, HELD):
                load_x(k)
            sp.wait_ge(k_copied, 2)
            store_kernels(sp, 0)
            store_kernels(sp, 1)
            for k in range(HELD, EARLY // 2):
                load_x(k)
            sp.wait_ge(tail_out, 16)
            sp.wait_ge(k_out[0], 16)
            for s in range(G):
                sp.dma_start(toep[s], toep_source(s)).then_inc(toep_arrived[s], 16)
                if s >= 1 and EARLY // 2 + s - 1 < H // 2:
                    load_x(EARLY // 2 + s - 1)

            def reload_toep(t, steps=range(G)):
                for s in steps:
                    h = t * G + s
                    sp.wait_ge(t_ready, h - G + 1)
                    sp.dma_start(toep[s], toep_source(h)).then_inc(toep_arrived[s], 16)

            reload_toep(1, range(2))
            sp.wait_ge(k_out[1], 16)
            sp.dma_start(w_nat, weight.rearrange("(j p) l -> p j l", p=P)).then_inc(w_in, 16)
            reload_toep(1, range(2, G))
            sp.dma_start(bias_b[:, :], bias.rearrange("(a o) -> a o", a=1).to_broadcast((P, O))).then_inc(row_in, 16)
            sp.dma_start(asg_i[:, :], assignments.rearrange("(a o) -> a o", a=1).to_broadcast((NC, O))).then_inc(row_in, 16)
            with sp.Fori(2, UT) as t:
                reload_toep(t)

            def reload_x(p, h):
                sp.dma_start(x_in[p], x[:, h:h + 2, :]).then_inc(x_back[p], 16)

            sp.wait_ge(ut_ready, H)
            for p in range(XB):
                reload_x(p, 2 * p)
            sp.wait_ge(wt_ready, J + 1)

            def load_xw(t):
                h = t * G
                sp.dma_start(xw[:, bass.ds(h - U, G), :], x[:, bass.ds(h, G), :]).then_inc(xw_back, 16)

            reload_toep(UT)
            load_xw(UT)
            with sp.Fori(UT + 1, T) as t:
                reload_toep(t)
                sp.wait_ge(xw_back, (t - UT) * 16)
                load_xw(t)
            sp.wait_ge(t_ready, H)
            sp.dma_start(x_last[:, :, :], x[:, U - G:U, :]).then_inc(x_last_back, 16)
            for h in range(0, U - G, 2):
                for k in (2 * h, 2 * h + 2):
                    if k < H - U:
                        sp.wait_ge(result_w_ready, k // 2 + 1)
                        sp.dma_start(out[:, U + k:U + k + 2, :], xy[:, U + k:U + k + 2, :]).then_inc(stored, 16)
                sp.wait_ge(result_ready, h + 2)
                sp.dma_start(out[:, h:h + 2, :], xy[:, h:h + 2, :]).then_inc(stored, 16)
                if h < U - G - 2 * XB:
                    reload_x(h // 2, h + 2 * XB)
            stores = (H - U) // 2 + (U - G) // 2 + G + 1
            for s in range(G - 1):
                sp.wait_ge(result_ready, U - G + s + 1)
                sp.dma_start(out[:, U - G + s, :], xy[:, U - G + s, :]).then_inc(stored, 16)
            for i in range(2):
                half = slice(i * OH, (i + 1) * OH)
                sp.wait_ge(result_last_ready, i + 1)
                sp.dma_start(out[:, U - 1, half], xy[:, U - 1, half]).then_inc(stored, 16)
            sp.wait_ge(stored, 16 * stores)

        @block.gpsimd
        def _(pool):
            made = [0]

            def link(ins):
                made[0] += 1
                ins.then_inc(pool_step, 1)
                pool.wait_ge(pool_step, made[0])

            link(pool.memset(ident[:, :], 0.0))
            pool.affine_select(out=ident[:, :], in_=ident[:, :], compare_op=ALU.not_equal, fill=1.0, base=0,
                               pattern=[[-1, P]], channel_multiplier=1).then_inc(consts, 1)
            pool.iota(lval[:, 0:LC], [[-1, LC]], base=LC - 1, channel_multiplier=0,
                      allow_small_or_imprecise_dtypes=True).then_inc(consts, 1)
            pool.iota(lval[:, LC:LV], [[-LC, LA]], base=L - LC, channel_multiplier=0,
                      allow_small_or_imprecise_dtypes=True).then_inc(consts, 1)
            pool.memset(zero[:, :], 0.0).then_inc(consts, 1)
            pool.memset(half_pi[:, :], math.pi / 2).then_inc(consts, 1)
            pool.iota(pos[:, :], [[P, J]], base=P - 1, channel_multiplier=-1,
                      allow_small_or_imprecise_dtypes=True).then_inc(consts, 1)
            pool.iota(clus[:, :], [[0, 1]], base=0, channel_multiplier=1,
                      allow_small_or_imprecise_dtypes=True).then_inc(consts, 1)
            pool.memset(best[:, :, :], 0.0).then_inc(best_ready, 1)
            pool.memset(g_a, 0.0).then_inc(g_zero, 1)
            link(pool.memset(d_at0[:, :], 0.0))
            for i in range(2):
                pool.dma_start(d_at0[(i + 1) * LA - 1:(i + 1) * LA, :],
                               D[i * HH:(i + 1) * HH].rearrange("(a h) -> a h", a=1)).then_inc(d_in, 16)
            pool.wait_ge(dta_ready, 1)
            pool.tensor_tensor(grow, dta_r[:, :].unsqueeze(2).to_broadcast((P, HH, LV)),
                               lval[:, :].unsqueeze(1).to_broadcast((P, HH, LV)), ALU.mult).then_inc(grow_ready, 1)
            pool.wait_ge(osc_ready, 2)
            pool.wait_ge(mag_ready, 1)
            for i in range(2):
                pool.tensor_tensor(f_c[:, i, :, :], osc[:, i, :, 0:LC], mag[:, :, 0:LC], ALU.mult).then_inc(f_ready, 1)
            pool.wait_ge(e_pq_ready, 1)
            pool.tensor_tensor(g_a[0:N, 0, :, 0:LA], e_p[0:N, 0, :, :], e_q[0:N, 1, :, :], ALU.subtract).then_inc(g_ready, 1)
            pool.wait_ge(cen_in, 16)
            for j in range(J):
                pool.tensor_copy(cen_rev[:, j * P:(j + 1) * P], cen_nat[:, back(j)]).then_inc(rev_ready, 1)

            def low_t(h, s):
                pool.wait_ge(t_hi_ready, h + 1)
                pool.tensor_tensor(t_lo[s][:, :], toep[s], t_hi[s][:, :].bitcast(F32), ALU.subtract).then_inc(t_ready, 1)

            def probabilities(t):
                hs = slice(t * G, t * G + G) if isinstance(t, int) else bass.ds(t * G, G)
                pool.wait_ge(inv_ready, t + 1)
                pool.tensor_tensor(prob[:, :, :], e[:, :, :], inv[:, hs].unsqueeze(2).to_broadcast((P, G, NC)),
                                   ALU.mult).then_inc(prob_ready, 1)

            def low_y(n, y, s):
                pool.wait_ge(y_hi_ready, n + 1)
                pool.tensor_tensor(y_lo[s], y, y_hi[s].bitcast(F32), ALU.subtract).then_inc(y_split, 1)

            pool.wait_ge(t_ready, 1)
            for s in range(1, 3):
                low_t(s, s)
            for s in range(G):
                low_t(s + 3, (s + 3) % G)
            with pool.Fori(1, UT) as t:
                for s in range(G):
                    if s == 2:
                        probabilities(t - 1)
                    low_t(t * G + s + 3, (s + 3) % G)

            def channels(t, last=False):
                for s in range(G):
                    low_y(t * G + s - U, y_m[s % 2][:, :], s)
                    if not (last and s > 0):
                        low_t(t * G + s + 3, (s + 3) % G)
                    if s == 2:
                        probabilities(t - 1)

            with pool.Fori(UT, T - 1) as t:
                channels(t)
            channels(T - 1, True)

            LEAD = G + 2

            def residual(h):
                if h < U - G:
                    x_h = x_in[h // 2 % XB][:, h % 2, :]
                    pool.wait_ge(x_back[h // 2 % XB], 16 * (h // (2 * XB) + 1))
                else:
                    x_h = x_last[:, h - U + G, :]
                    pool.wait_ge(x_last_back, 16)
                pool.wait_ge(chosen_ready, h + 1)
                pool.tensor_tensor(xy[:, h, :], xy[:, h, :], x_h, ALU.add).then_inc(result_ready, 1)

            for s in range(2):
                low_y(H - U + s, xy[:, s, :], s)
            probabilities(T - 1)
            for h in range(2, LEAD):
                low_y(H - U + h, xy[:, h, :], h % G)
            for h in range(U - 1):
                residual(h)
                if h + LEAD < U:
                    low_y(H - U + h + LEAD, xy[:, h + LEAD, :], (h + LEAD) % G)

        @block.scalar
        def _(act):
            act.dma_start(aim_n[:, :, :], A_imag.rearrange("(a h) n -> h a n", a=2)).then_inc(par_in, 16)
            act.dma_start(ex[:, 1, :], bass.AP(log_dt.tensor, log_dt.offset, [[HH, 2], [0, N], [1, HH]])).then_inc(dt_in, 16)
            act.preload_act_table_set("exp_and_others")

            def keep_u(h):
                act.wait_ge(ut_ready, h + 1)
                act.activation(xy[:, h, :], xt[h % XT][:, :], ACT.Copy).then_inc(ut_kept[h % XT], 1)

            for h in ACT_KEEPS[0]:
                keep_u(h)
            act.wait_ge(dta_ready, 1)
            act.activation(th[:, :], dta_r[:, :], ACT.Tanh, scale=0.5).then_inc(small_ready, 1)
            act.wait_ge(grow_ready, 1)
            act.activation(mag, grow, ACT.Exp).then_inc(mag_ready, 1)
            act.wait_ge(turn_ready, 1)
            act.activation(s1[:, :], frac[:, :], ACT.Sin, scale=TWO_PI).then_inc(small_ready, 1)
            act.activation(sh[:, :], frac[:, :], ACT.Sin, scale=TWO_PI / 2).then_inc(small_ready, 1)
            act.wait_ge(phase_ready, 1)
            act.activation(osc[:, 1, :, :], phase, ACT.Sin, scale=TWO_PI).then_inc(osc_ready, 1)
            act.wait_ge(phase_ready, 2)
            act.wait_ge(consts, 5)
            act.activation(osc[:, 0, :, :], absph, ACT.Sin, scale=-TWO_PI, bias=half_pi[:, :]).then_inc(osc_ready, 1)
            for h in ACT_KEEPS[1]:
                keep_u(h)
            act.preload_act_table_set("exp_and_others")

            def high_u(h, s, first=False):
                if not first:
                    act.wait_ge(conv_done, h - 1)
                act.activation(u_hi[s % 2][:, :], xy[:, h, :], ACT.Copy).then_inc(u_hi_ready, 1)

            for s in range(2):
                act.wait_ge(ut_kept[s], 1)
                high_u(s, s, True)
            act.wait_ge(d_added, 1)
            act.activation(k_sb[:, 0:KH], spare[0][0:2 * LA, 0:KH], ACT.Copy).then_inc(k_copied, 1)

            def high_t(t, s, first=False):
                h = t * G + s
                act.wait_ge(toep_arrived[s], 16 * (t + 1))
                if not first:
                    act.wait_ge(conv_done, h - G + 1)
                act.activation(t_hi[s][:, :], toep[s], ACT.Copy).then_inc(t_hi_ready, 1)

            for h in ACT_KEEPS[2]:
                if h == ACT_KEEPS[2][-2]:
                    high_t(0, 0, True)
                keep_u(h)

            def keep_y(h, s):
                act.activation(xy[:, h, :], y_m[s % 2][:, :], ACT.Copy).then_inc(y_kept, 1)

            def exps(t):
                act.wait_ge(above_ready, t + 1)
                if not (isinstance(t, int) and t == 0):
                    act.wait_ge(prob_ready, t)
                act.activation(e[:, :, :], above[:, :, :], ACT.Exp, scale=1.0 / TEMPERATURE).then_inc(e_ready, 1)

            def high_y(y, s):
                act.activation(y_hi[s], y, ACT.Copy).then_inc(y_hi_ready, 1)

            act.wait_ge(wt_ready, 1)
            act.activation(cenT[:, :, :], yt[1][:, 0:J * NC].rearrange("p (j c) -> p j c", c=NC), ACT.Copy).then_inc(cen_copied, 1)
            for s in range(1, 3):
                high_t(0, s, True)

            def channels(t):
                for s in range(G):
                    high_u(t * G + s + 2, s)
                    if s == 1 and not (isinstance(t, int) and t == 0):
                        exps(t - 1)
                    for i in LATE[s] if isinstance(t, int) and t == 0 else ():
                        if i % 2 == 0:
                            act.wait_ge(ut_ready, EARLY + i + 1)
                            act.activation(xy[:, EARLY + i, :], ut[0], ACT.Copy).then_inc(ut_kept[0], 1)
                    if isinstance(t, int) and t == 0 and s == 0:
                        act.wait_ge(cen_copied, 1)
                        act.activation(w_hi[:, :, :, OH:], cen_halves, ACT.Copy).then_inc(cen_hi_ready, 1)
                    if isinstance(t, int) and t == 1:
                        act.wait_ge(wt_ready, s + 2)
                        act.activation(w_hi[:, s, :, 0:OH], duos[s], ACT.Copy).then_inc(w_hi_ready, 1)
                    act.wait_ge(y_ready, t * G + s + 1)
                    high_t(t + (s + 3) // G, (s + 3) % G, isinstance(t, int) and t == 0 and s == 0)
                    keep_y(t * G + s, s)
                    if isinstance(t, int) and t == 0 and s == 3:
                        act.wait_ge(w_in, 16)
                        act.activation(w_rev[:, :, s * P:], w_nat[:, :, back(s)], ACT.Copy).then_inc(w_rev_last_ready, 1)

            channels(0)
            channels(1)
            with act.Fori(2, UT) as t:
                channels(t)

            def channels_w(t, place):
                for s in range(G):
                    h = t * G + s
                    if not (place == "last" and s >= 2):
                        high_u(h + 2, s)
                    if place != "first":
                        act.wait_ge(duo_done, h - U - G + 1)
                    act.wait_ge(y_ready, h + 1)
                    high_y(y_m[s % 2][:, :], s)
                    if s == 1:
                        exps(t - 1)
                    if not (place == "last" and s > 0):
                        high_t(t + (s + 3) // G, (s + 3) % G)

            channels_w(UT, "first")
            with act.Fori(UT + 1, T - 1) as t:
                channels_w(t, "")
            channels_w(T - 1, "last")
            act.wait_ge(y_kept, U)
            for s in range(G):
                if s == G - 1:
                    exps(T - 1)
                act.wait_ge(duo_done, H - U - G + s + 1)
                high_y(xy[:, s, :], s)
            with act.Fori(1, UT) as t:
                for s in range(G):
                    act.wait_ge(dense_done, t * G + s - G + 1)
                    high_y(xy[:, t * G + s, :], s)

        @block.vector
        def _(dve):
            made = [0]

            def link(ins):
                made[0] += 1
                ins.then_inc(dve_step, 1)
                dve.wait_ge(dve_step, made[0])

            tt, ts, stt = nc.vector.tensor_tensor, nc.vector.tensor_scalar, nc.vector.scalar_tensor_tensor
            dve.wait_ge(params_t, 1)
            pt = yt[0][:, 0:4 * HH].rearrange("p (k h) -> p k h", h=HH)
            nc.vector.tensor_copy(ex[:, 0, :], pt[:, 0, :])
            link(nc.vector.tensor_copy(par[:, :, :], pt[:, 1:4, :]))
            dve.wait_ge(dt_in, 16)
            v = ex[:, :, :]
            kf, k, r, q, k2 = (tmp[i][:, :, :] for i in range(5))
            c = exp_coefficients()
            aim, c_re, c_im = par[:, 0, :], par[:, 1, :], par[:, 2, :]
            link(ts(v, v, -87.0, 88.0, ALU.max, ALU.min))
            link(ts(kf, v, 1.0 / math.log(2.0), MAGIC, ALU.mult, ALU.add))
            link(ts(k, kf, MAGIC, None, ALU.subtract))
            link(stt(r, k, -LN2_HI, v, ALU.mult, ALU.add))
            link(stt(r, k, -LN2_LO, r, ALU.mult, ALU.add))
            ts(k2.bitcast(I32), kf.bitcast(I32), MANTISSA, None, ALU.logical_shift_left)
            link(ts(q, r, c[-1], None, ALU.mult))
            for cj in c[-2::-1]:
                link(stt(q, q, cj, r, ALU.add, ALU.mult))
            link(ts(q, q, 1.0, None, ALU.add))
            link(tt(v.bitcast(I32), q.bitcast(I32), k2.bitcast(I32), ALU.add))
            e_re, dt = ex[:, 0, :], ex[:, 1, :]
            b, w2 = tmp[0][:, 0, :], tmp[0][:, 1, :]
            tt(b, aim, dt, ALU.mult)
            stt(dta_r[:, :], e_re, -1.0, dt, ALU.mult, ALU.mult).then_inc(dta_ready, 1)
            link(tt(abs2[:, 0, :], e_re, e_re, ALU.mult))
            ts(turns[:, :], b, 1.0 / (2 * math.pi), None, ALU.mult)
            link(tt(abs2[:, 1, :], aim, aim, ALU.mult))
            ts(w2, turns[:, :], MAGIC, MAGIC, ALU.add, ALU.subtract)
            link(tt(abs2[:, 0, :], abs2[:, 0, :], abs2[:, 1, :], ALU.add))
            tt(frac[:, :], turns[:, :], w2, ALU.subtract).then_inc(turn_ready, 1)
            recip, m1, m2, m3, m4, w_re, w_im, ea1, d1, cosm1, e_im, e_r = (small[:, i, :] for i in range(12))
            dve.wait_ge(consts, 3)
            tt(phase, turns[:, :].unsqueeze(2).to_broadcast((P, HH, LV)),
               lval[:, :].unsqueeze(1).to_broadcast((P, HH, LV)), ALU.mult)
            dve.wait_ge(small_ready, 1)
            ts(d1, th[:, :], -1.0, 1.0, ALU.mult, ALU.add)
            link(tt(m1, c_re, e_re, ALU.mult))
            ts(whole, phase, MAGIC, MAGIC, ALU.add, ALU.subtract)
            nc.vector.reciprocal(d1, d1)
            link(tt(m2, c_im, aim, ALU.mult))
            tt(phase, phase, whole, ALU.subtract).then_inc(phase_ready, 1)
            stt(ea1, th[:, :], 2.0, d1, ALU.mult, ALU.mult)
            link(tt(m1, m2, m1, ALU.subtract))
            ts(absph.bitcast(I32), phase.bitcast(I32), 0x7FFFFFFF, None, ALU.bitwise_and).then_inc(phase_ready, 1)
            tt(m3, c_re, aim, ALU.mult)
            tt(m4, c_im, e_re, ALU.mult)
            link(nc.vector.reciprocal(recip, abs2[:, 0, :]))
            dve.wait_ge(small_ready, 3)
            stt(e_im, ea1, 1.0, s1[:, :], ALU.add, ALU.mult)
            tt(m3, m3, m4, ALU.add)
            link(stt(cosm1, sh[:, :], -2.0, sh[:, :], ALU.mult, ALU.mult))
            stt(w_re, m1, 2.0, recip, ALU.mult, ALU.mult)
            link(stt(e_r, cosm1, 1.0, ea1, ALU.add, ALU.mult))
            stt(w_im, m3, -2.0, recip, ALU.mult, ALU.mult)
            link(tt(e_r, e_r, cosm1, ALU.add))
            tt(m1, e_r, w_re, ALU.mult)
            tt(m2, e_im, w_im, ALU.mult)
            tt(m3, e_r, w_im, ALU.mult)
            link(tt(m4, e_im, w_re, ALU.mult))
            dve.wait_ge(osc_ready, 2)
            dve.wait_ge(mag_ready, 1)
            tt(e_a, osc[:, :, :, LC:LV], mag[:, :, LC:LV].unsqueeze(1).to_broadcast((P, 2, HH, LA)), ALU.mult)
            tt(coef[:, 0, :], m1, m2, ALU.subtract)
            link(tt(coef[:, 1, :], m3, m4, ALU.add))
            for e_c, k in ((e_p, 0), (e_q, 1)):
                last = tt(e_c, e_a, coef[:, k, :].unsqueeze(1).unsqueeze(3).to_broadcast((P, 2, HH, LA)), ALU.mult)
            last.then_inc(e_pq_ready, 1)
            dve.wait_ge(e_pq_ready, 1)
            dve.wait_ge(g_zero, 1)
            tt(g_a[N:P, 0, :, LA:2 * LA], e_p[N:P, 0, :, :], e_q[N:P, 1, :, :], ALU.subtract)
            for a in range(2):
                own = slice(a * N, (a + 1) * N)
                last = stt(g_a[own, 1, :, a * LA:(a + 1) * LA], e_p[own, 1, :, :], -1.0, e_q[own, 0, :, :], ALU.mult, ALU.subtract)
            last.then_inc(g_ready, 1)

            def keep_u(h):
                dve.wait_ge(ut_ready, h + 1)
                nc.vector.tensor_copy(xy[:, h, :], xt[h % XT][:, :]).then_inc(ut_kept[h % XT], 1)

            dve.wait_ge(len_in, 16)
            dve.wait_ge(consts, 7)
            link(nc.vector.tensor_copy(len_f[:, :], len_i[:, :]))
            for j in range(J):
                ts(mask[:, j, :], len_f[:, :], pos[:, j:j + 1], None, ALU.is_gt).then_inc(mask_ready, 1)
            mask_f = mask[:, :, :].rearrange("p j b -> p (j b)")
            dve.wait_ge(k_ready, 1)
            dve.wait_ge(d_in, 32)
            for i in range(2):
                at0 = spare[i][0:2 * LA, 0:KH].rearrange("a (h c) -> a h c", c=LC)[:, :, LC - 1]
                tt(at0, at0, d_at0[:, i * HQ:(i + 1) * HQ], ALU.add).then_inc(d_added, 1)
            dve.wait_ge(d_added, 2)
            nc.vector.tensor_copy(k_sb[:, KH:], spare[1][0:2 * LA, 0:KH]).then_inc(k_copied, 1)

            def low_u(h, s):
                dve.wait_ge(u_hi_ready, h + 1)
                tt(u_lo[s % 2][:, :], xy[:, h, :], u_hi[s % 2][:, :].bitcast(F32), ALU.subtract).then_inc(u_ready, 1)

            for h in DVE_KEEPS:
                if h == DVE_KEEPS[2]:
                    low_u(0, 0)
                    low_u(1, 1)
                if h == DVE_KEEPS[-1]:
                    dve.wait_ge(t_hi_ready, 1)
                    tt(t_lo[0][:, :], toep[0], t_hi[0][:, :].bitcast(F32), ALU.subtract).then_inc(t_ready, 1)
                keep_u(h)
            dve.wait_ge(mask_ready, J)

            def mask_y(h, s, first=False, split=False):
                dve.wait_ge(conv_done, h + 1)
                if split:
                    dve.wait_ge(y_split, h - U - 1)
                elif not first:
                    dve.wait_ge(logits_done, h - 1)
                    dve.wait_ge(y_kept, h - 1)
                tt(y_m[s % 2][:, :], yt[s % 2][:, :], mask_f, ALU.mult).then_inc(y_ready, 1)

            logits_ps = lg[0][:, 0:G * NC].rearrange("p (g c) -> p g c", c=NC)
            base = made[0]

            def softmax_above(t, hs, from_sb=False):
                if from_sb:
                    dve.wait_ge(taken, (t - UT + 1) * G)
                else:
                    dve.wait_ge(logits_done, (t + 1) * G)
                logits = logits_sb[:, :, :] if from_sb else logits_ps
                nc.vector.reduce_max(top[:, hs], logits, AX.X).then_inc(dve_step, 1)
                dve.wait_ge(dve_step, base + 2 * t + 1)
                tt(above[:, :, :], logits, top[:, hs].unsqueeze(2).to_broadcast((P, G, NC)),
                   ALU.subtract).then_inc(above_ready, 1)

            def softmax_sum(t, hs):
                dve.wait_ge(e_ready, t + 1)
                nc.vector.reduce_sum(total[:, hs], e[:, :, :], AX.X).then_inc(dve_step, 1)
                dve.wait_ge(dve_step, base + 2 * t + 2)
                nc.vector.reciprocal(inv[:, hs], total[:, hs]).then_inc(inv_ready, 1)

            def queries(t, hs):
                dve.wait_ge(inv_ready, t + 1)
                ts(query[:, hs], inv[:, hs], THRESHOLD, None, ALU.is_gt).then_inc(query_ready, 1)

            def softmax_best(t):
                dve.wait_ge(prob_ready, t + 1)
                dve.wait_ge(best_ready, t + 1)
                tt(best[:, :, :], best[:, :, :], prob[:, :, :], ALU.max).then_inc(best_ready, 1)

            def reverse_w(j):
                dve.wait_ge(w_in, 16)
                nc.vector.tensor_copy(w_rev[:, :, j * P:(j + 1) * P], w_nat[:, :, back(j)]).then_inc(w_rev_ready, 1)

            for s in range(G):
                mask_y(s, s, s < 2)
                low_u(s + 2, s)
                for i in LATE[s]:
                    if i % 2 == 1:
                        dve.wait_ge(ut_ready, EARLY + i + 1)
                        nc.vector.tensor_copy(xy[:, EARLY + i, :], ut[1]).then_inc(ut_kept[1], 1)
                if s == 0:
                    dve.wait_ge(cen_hi_ready, 1)
                    tt(w_lo[:, :, :, OH:], cen_halves, w_hi[:, :, :, OH:].bitcast(F32), ALU.subtract).then_inc(w_lo_ready, 1)
                if s >= 2:
                    reverse_w(s - 2)

            def channels(t, hs):
                for s in range(G):
                    mask_y(t * G + s, s)
                    low_u(t * G + s + 2, s)
                    if s == 0:
                        softmax_above(t - 1, hs)
                    if s == 1:
                        softmax_sum(t - 1, hs)
                    if s == 2:
                        queries(t - 1, hs)
                        softmax_best(t - 1)
                    if isinstance(t, int):
                        if s == 0:
                            reverse_w(2)
                        if s == 3:
                            dve.wait_ge(row_in, 32)
                            dve.wait_ge(consts, 7)
                            nc.vector.tensor_copy(asg_f[:, :], asg_i[:, :]).then_inc(asg_ready, 1)
                            dve.wait_ge(asg_ready, 1)
                            ts(onehot[:, :], asg_f[:, :], clus[:, :], None, ALU.is_equal)
                        dve.wait_ge(w_hi_ready, s + 1)
                        tt(w_lo[:, s, :, 0:OH], duos[s], w_hi[:, s, :, 0:OH].bitcast(F32),
                           ALU.subtract).then_inc(w_lo_ready, 1)

            channels(1, slice(0, G))
            with dve.Fori(2, UT) as t:
                channels(t, bass.ds(t * G - G, G))

            def take(n, s, h):
                dve.wait_ge(duo_done, n + 1)
                tt(xy[:, h, :].rearrange("p (i o) -> p i o", i=2), duo[s % 2][:, :, 0:OH], bias_halves, ALU.add)
                nc.vector.tensor_copy(logits_sb[:, s, :].rearrange("p (i c) -> p i c", i=2), duo[s % 2][:, :, OH:OH + CH]).then_inc(taken, 1)

            def channels_w(t, hs, place=""):
                first, last = place == "first", place == "last"
                for s in range(G):
                    h = t * G + s
                    mask_y(h, s, split=not (first and s < 2))
                    if not (last and s >= 2):
                        low_u(h + 2, s)
                    if s == 1:
                        softmax_sum(t - 1, hs)
                    if s == 2:
                        queries(t - 1, hs)
                    if not first and s >= 2:
                        mix(t - 1, 2 * s - 4)
                        mix(t - 1, 2 * s - 3)
                    if not (first and s == 0):
                        take(h - 1 - U, (s - 1) % G, h - 1)
                    if s == 3:
                        softmax_best(t - 1)
                    if s == 0:
                        softmax_above(t - 1, hs, not first)
                        dve.wait_ge(above_ready, t)

            def mix(t, s):
                h = t * G + s
                dve.wait_ge(query_ready, t + 1)
                dve.wait_ge(taken, h - U + 1)
                dve.wait_ge(xw_back, (t - UT + 1) * 16)
                stt(xy[:, h, :], xy[:, h, :], query[:, bass.ds(h, 1)], xw[:, bass.ds(h - U, 1), :].rearrange("p a o -> p (a o)"),
                    ALU.mult, ALU.add).then_inc(mixed, 1)

            bias_halves = bias_b[:, :].rearrange("p (i o) -> p i o", i=2)
            channels_w(UT, slice(U - G, U), "first")
            with dve.Fori(UT + 1, T - 1) as t:
                channels_w(t, bass.ds(t * G - G, G))
            channels_w(T - 1, slice(H - 2 * G, H - G), "last")
            take(H - 1 - U, G - 1, H - 1)
            hs = slice(H - G, H)
            softmax_above(T - 1, hs, True)
            softmax_sum(T - 1, hs)
            queries(T - 1, hs)
            softmax_best(T - 1)
            made[0] = base + 2 * T
            dve.wait_ge(best_ready, T + 1)
            nc.vector.reduce_max(best1[:, :], best[:, :, :].rearrange("p g c -> p c g"), AX.X).then_inc(sel_ready, 1)

            def add_bias(h, s):
                dve.wait_ge(dense_done, h + 1)
                tt(xy[:, h, :], bank[s], bias_b[:, :], ALU.add).then_inc(dense_read, 1)

            def choose(h):
                dve.wait_ge(dense_read, h + 1)
                stt(xy[:, h, :], xy[:, h, :], query[:, bass.ds(h, 1)], rows, ALU.mult, ALU.mult).then_inc(chosen_ready, 1)

            mix(T - 1, 0)
            dve.wait_ge(best_t, 1)
            link(nc.vector.reduce_max(best_c[:, :], yt[0][0:NC, 0:P], AX.X))
            ts(sel_b[:, :], best_c[:, :].to_broadcast((NC, P)), THRESHOLD, None, ALU.is_gt).then_inc(sel_ready, 1)
            add_bias(0, 0)
            for s in range(1, G):
                mix(T - 1, s)
            add_bias(1, 1)
            dve.wait_ge(rows_ps, 1)
            ts(not_rows[:, :], rows, 0.0, None, ALU.is_equal).then_inc(not_rows_ready, 1)
            dve.wait_ge(not_rows_ready, 1)
            dve.wait_ge(mixed, H - U)

            def pass_x(k):
                nc.vector.copy_predicated(xy[:, U + k:U + k + 2, :], not_rows[:, :].unsqueeze(1).to_broadcast((P, 2, O)),
                                          xw[:, k:k + 2, :]).then_inc(result_w_ready, 1)

            last_x = x_last[:, G - 1, :]
            q_last = query[:, U - 1:U]
            for h in range(U - G):
                if h < U - G - 2:
                    add_bias(h + 2, (h + 2) % G)
                choose(h)
                if 2 * h < H - U:
                    pass_x(2 * h)
                if 2 * h == H - U:
                    nc.vector.tensor_copy(rows_sb, rows)
                if 2 * h == H - U + 2:
                    stt(last_bias, bias_b[:, :], q_last, rows, ALU.mult, ALU.mult).then_inc(last_ready, 1)
            for s in range(G - 1):
                h = U - G + s
                if s == 0:
                    dve.wait_ge(last_ready, 1)
                    dve.wait_ge(x_last_back, 16)
                    tt(last_x, last_x, last_bias, ALU.add).then_inc(last_ready, 1)
                add_bias(h, s)
                choose(h)
            for i in range(2):
                half = slice(i * OH, (i + 1) * OH)
                dve.wait_ge(dense_done, U + i)
                stt(xy[:, U - 1, half], last_half[i], q_last, rows_sb[:, half], ALU.mult, ALU.mult).then_inc(last_ready, 1)
                dve.wait_ge(last_ready, i + 3)
                tt(xy[:, U - 1, half], xy[:, U - 1, half], last_x[:, half], ALU.add).then_inc(result_last_ready, 1)

        @block.tensor
        def _(pe):
            mm, tr = nc.tensor.matmul, nc.tensor.transpose
            pe.wait_ge(consts, 1)
            pe.wait_ge(par_in, 48)
            flat = "h a n -> h (a n)"
            for i, src in enumerate((lar_n[:, :, :].rearrange(flat), aim_n[:, :, :].rearrange(flat),
                                     c_n[:, :, :, 0].rearrange(flat), c_n[:, :, :, 1].rearrange(flat))):
                last = tr(yt[0][:, i * HH:(i + 1) * HH], src, ident[0:HH, 0:HH])
            last.then_inc(params_t, 1)

            def transposes(h, to):
                pe.wait_ge(x_arrived[h // 2 % XS], 16 * (h // (2 * XS) + 1))
                for j in range(J):
                    last = tr(to[:, j * P:(j + 1) * P], x_in[h // 2 % XS][:, h % 2, j * P:(j + 1) * P], ident[:, :])
                last.then_inc(ut_ready, 1)

            def early_transposes(channels):
                for h in channels:
                    if h == 4:
                        pe.wait_ge(dta_ready, 1)
                    if h >= XT:
                        pe.wait_ge(ut_kept[h % XT], h // XT)
                    transposes(h, xt[h % XT])

            early_transposes(range(BEFORE_K))
            pe.wait_ge(f_ready, 2)
            pe.wait_ge(g_ready, 2)
            for g in range(HH):
                for i in range(2):
                    last = mm(spare[g // HQ][0:2 * LA, g % HQ * LC:(g % HQ + 1) * LC], g_a[:, i, g, :], f_c[:, i, g, :],
                              start=(i == 0), stop=(i == 1))
            last.then_inc(k_ready, 1)
            early_transposes(range(BEFORE_K, EARLY))
            pe.wait_ge(rev_ready, J)
            pe.wait_ge(ut_kept[5], KEPT_EARLY[5])
            for j in range(J):
                last = tr(yt[1][:, j * NC:(j + 1) * NC], cen_rev[:, j * P:(j + 1) * P], ident[0:NC, 0:NC])
            last.then_inc(wt_ready, 1)

            def convolution(t, s, first=False):
                h = t * G + s
                pe.wait_ge(u_ready, h + 1)
                pe.wait_ge(t_ready, h + 1)
                if not first:
                    pe.wait_ge(y_ready, h - 1)
                for d in range(J):
                    blocks = slice((J - 1 - d) * P, (J - d) * P)
                    for i, (tp, u) in enumerate(((t_hi, u_hi), (t_hi, u_lo), (t_lo, u_hi))):
                        last = mm(yt[s % 2][:, d * P:], tp[s][:, blocks], u[s % 2][:, 0:(J - d) * P],
                                  start=(d == 0 and i == 0), stop=(d == J - 1 and i == 2))
                last.then_inc(conv_done, 1)

            def logits(h, s):
                pe.wait_ge(y_ready, h + 1)
                for j in range(J):
                    last = mm(lg[0][:, s * NC:(s + 1) * NC], y_m[s % 2][:, j * P:(j + 1) * P], cenT[:, j, :],
                              start=(j == 0), stop=(j == J - 1))
                last.then_inc(logits_done, 1)

            pe.wait_ge(ut_kept[4], KEPT_EARLY[4])
            for s in range(G):
                convolution(0, s, s < 2)
                if s == 0:
                    pe.wait_ge(cen_copied, 1)
                    pe.wait_ge(ut_kept[2], KEPT_EARLY[2])
                else:
                    logits(s - 1, s - 1)
                for i in LATE[s]:
                    pe.wait_ge(ut_kept[i % 2], KEPT_EARLY[i % 2] + i // 2)
                    transposes(EARLY + i, ut[i % 2])

            def channels(t):
                for s in range(G):
                    if isinstance(t, int):
                        if s < J - 1:
                            pe.wait_ge(w_rev_ready, s + 1)
                        else:
                            pe.wait_ge(w_rev_last_ready, 1)
                        if s >= 2:
                            pe.wait_ge(ut_kept[s - 2], KEPT_EARLY[s - 2] + (late + 3 - s) // 2)
                        for o in range(O // P):
                            last = tr(bank[s][:, o * P:(o + 1) * P], w_rev[:, o, s * P:(s + 1) * P], ident[:, :])
                        last.then_inc(wt_ready, 1)
                    convolution(t, s)
                    if s == 1:
                        pe.wait_ge(above_ready, t)
                    logits(t * G + s - 1, (s - 1) % G)

            pe.wait_ge(k_copied, 2)
            channels(1)
            with pe.Fori(2, UT) as t:
                channels(t)

            def layer_and_logits(n, s, first=False):
                pe.wait_ge(y_split, n + 1)
                if not first:
                    pe.wait_ge(taken, n - 1)
                for j in range(J):
                    js = slice(j * P, (j + 1) * P)
                    for k, (y, w) in enumerate(((y_hi, w_hi), (y_hi, w_lo), (y_lo, w_hi))):
                        for i in range(2):
                            last = mm(duo[s % 2][:, i, 0:OH + CH], y[s][:, js], w[:, j, i, :],
                                      start=(j == 0 and k == 0), stop=(j == J - 1 and k == 2))
                last.then_inc(duo_done, 1)

            for s in range(G):
                convolution(UT, s)
                if s == 0:
                    logits(U - 1, G - 1)
                    pe.wait_ge(w_lo_ready, J + 1)
                else:
                    layer_and_logits(s - 1, s - 1, s <= 2)
            with pe.Fori(UT + 1, T) as t:
                for s in range(G):
                    convolution(t, s)
                    layer_and_logits(t * G + s - 1 - U, (s - 1) % G)
            layer_and_logits(H - 1 - U, G - 1)

            def layer(h, s, first=False, between=None):
                pe.wait_ge(y_split, h + (H - U) + 1)
                if first:
                    pe.wait_ge(taken, H - U - 1 + s // 2)
                else:
                    pe.wait_ge(dense_read, h - G + 1)
                for j in range(J):
                    if j == J // 2 and between:
                        between()
                    js = slice(j * P, (j + 1) * P)
                    mm(duos[s], y_hi[s][:, js], w_hi[:, j, :, 0:OH], start=(j == 0), stop=False)
                    mm(duos[s], y_hi[s][:, js], w_lo[:, j, :, 0:OH], start=False, stop=False)
                    last = mm(duos[s], y_lo[s][:, js], w_hi[:, j, :, 0:OH], start=False, stop=(j == J - 1))
                last.then_inc(dense_done, 1)

            layer(0, 0, True)

            def transpose_best():
                pe.wait_ge(sel_ready, 1)
                tr(yt[0][0:NC, 0:P], best1[:, :], ident[:, :]).then_inc(best_t, 1)

            def select_rows():
                pe.wait_ge(sel_ready, 2)
                mm(yt[1][:, :], sel_b[:, :], onehot[:, :], start=True, stop=True).then_inc(rows_ps, 1)

            layer(1, 1, True)
            transpose_best()
            layer(2, 2, True, select_rows)
            layer(3, 3, True)
            with pe.Fori(1, UT - 1) as t:
                for s in range(G):
                    layer(t * G + s, s)
            for s in range(G - 1):
                layer(U - G + s, s)
            pe.wait_ge(y_split, H)
            for i in range(2):
                pe.wait_ge(dense_read, U - G + i)
                for j in range(J):
                    for k, (y, w) in enumerate(((y_hi, w_hi), (y_hi, w_lo), (y_lo, w_hi))):
                        last = mm(last_half[i], y[G - 1][:, j * P:(j + 1) * P], w[:, j, i, 0:OH],
                                  start=(j == 0 and k == 0), stop=(j == J - 1 and k == 2))
                last.then_inc(dense_done, 1)


_INS = ["x", "itok_B_8_3872", "L0_cond_log_dt", "L0_cond_C", "L0_cond_log_A_real", "L0_cond_A_imag", "L0_cond_D",
        "L0_ffn_weight", "L0_ffn_bias", "L0_ffn_centroids", "L0_ffn_assignments"]


def kernel(**inputs):
    import numpy as _np
    import concourse.bacc as _bacc
    from concourse import mybir as _mybir
    from concourse.bass_utils import run_bass_kernel_spmd as _run

    nc = _bacc.Bacc("TRN2", target_bir_lowering=False, num_devices=1)
    arrays, args = {}, []
    for name in _INS:
        a = _np.ascontiguousarray(inputs[name])
        arrays[f"in_{name}"] = a
        args.append(nc.dram_tensor(f"in_{name}", a.shape, _mybir.dt.from_np(a.dtype), kind="ExternalInput").ap())
    out = nc.dram_tensor("out_0", (P, H, L), _mybir.dt.float32, kind="ExternalOutput").ap()
    program(nc, *args, out)
    r = _run(nc, [arrays], core_ids=[0])
    return r.results[0]["out_0"]
```
